# Optimizing a Trainium2 kernel written in Bass

```python
import numpy as np
import jax
import jax.numpy as jnp

def _softmax(x, axis=-1):
    return jax.nn.softmax(x, axis=axis)

def _gelu(x):
    return jax.nn.gelu(x, approximate=True)

def _silu(x):
    return jax.nn.silu(x)

def _sigmoid(x):
    return jax.nn.sigmoid(x)

def _layernorm(x, axis=-1, eps=1e-05):
    m = jnp.mean(x, axis=axis, keepdims=True)
    v = jnp.var(x, axis=axis, keepdims=True)
    return (x - m) / jnp.sqrt(v + eps)

def _scatter_add(tgt, idx, src, axis=0):
    return tgt.at[idx].add(src)

def _segment_sum(src, seg, n):
    return jax.ops.segment_sum(src, seg, n)
kernel_name = 'mk_gnn_preln_d1_gnn_r32_c5feb2'

def setup_inputs(seed: int=0):
    np.random.seed(seed)
    _w = jnp.asarray

    def _rec_inputs():
        import jax
        import jax.numpy as jnp
        _gk = jax.random.key(seed)
        x = -0.000202 + 1 * jax.random.normal(jax.random.fold_in(_gk, 1), (3125, 128), jnp.float32)
        src = jax.random.randint(jax.random.fold_in(_gk, 2), (50000,), 0, 3125, jnp.int32)
        dst = jax.random.randint(jax.random.fold_in(_gk, 3), (50000,), 0, 3125, jnp.int32)
        _o = jnp.argsort(dst, stable=True)
        src = src[_o]
        dst = dst[_o]
        edge_type_16 = jax.random.randint(jax.random.fold_in(_gk, 12), (50000,), 0, 16, jnp.int32)
        node_type_8 = jax.random.randint(jax.random.fold_in(_gk, 13), (3125,), 0, 8, jnp.int32)
        return (x, src, dst, edge_type_16, node_type_8)
    x, src, dst, edge_type_16, node_type_8 = _rec_inputs()

    def _L0_gnn_setup():
        import jax, jax.numpy as jnp
        import numpy as np
        N_NODES = 50000
        N_EDGES = 20000
        D = 128
        N_RELS = 16
        N_NTYPES = 8
        key = jax.random.key(seed)
        ks = jax.random.split(key, 9)
        return {'feats': jax.random.normal(ks[0], (N_NODES, D), dtype=jnp.float32), 'W_edge': jax.random.normal(ks[1], (N_RELS, D, D), dtype=jnp.float32) / np.sqrt(D), 'b_edge': jax.random.normal(ks[2], (N_RELS, D), dtype=jnp.float32) * 0.02, 'W_node': jax.random.normal(ks[3], (N_NTYPES, D, D), dtype=jnp.float32) / np.sqrt(D), 'b_node': jax.random.normal(ks[4], (N_NTYPES, D), dtype=jnp.float32) * 0.02, 'src': jax.random.randint(ks[5], (N_EDGES,), 0, N_NODES, dtype=jnp.int32), 'dst': jax.random.randint(ks[6], (N_EDGES,), 0, N_NODES, dtype=jnp.int32), 'ntypes': jax.random.randint(ks[7], (N_NODES,), 0, N_NTYPES, dtype=jnp.int32), 'etypes': jax.random.randint(ks[8], (N_EDGES,), 0, N_RELS, dtype=jnp.int32)}
    _L0_gnn_all = _L0_gnn_setup()
    _L0_gnn_in = {k: v for k, v in _L0_gnn_all.items() if k in ('W_edge', 'b_edge', 'W_node', 'b_node')}
    del _L0_gnn_all
    return {'x': x, 'src': src, 'dst': dst, 'edge_type_16': edge_type_16, 'node_type_8': node_type_8, 'L0_gnn_W_edge': _L0_gnn_in['W_edge'], 'L0_gnn_b_edge': _L0_gnn_in['b_edge'], 'L0_gnn_W_node': _L0_gnn_in['W_node'], 'L0_gnn_b_node': _L0_gnn_in['b_node']}

def reference(x, src, dst, edge_type_16, node_type_8, L0_gnn_W_edge, L0_gnn_b_edge, L0_gnn_W_node, L0_gnn_b_node):
    import jax
    import jax.numpy as jnp

    def _L0_gnn_ref(feats, W_edge, b_edge, W_node, b_node, src, dst, ntypes, etypes):
        import jax, jax.numpy as jnp
        import numpy as np
        N_NODES = 50000
        N_EDGES = 20000
        D = 128
        N_RELS = 16
        N_NTYPES = 8
        N, d = feats.shape
        T = W_edge.shape[0]
        hW = jnp.einsum('nd,tdf->tnf', feats, W_edge) + b_edge[:, None, :]
        msg = hW[etypes, src]
        seg = dst * T + etypes
        counts = jax.ops.segment_sum(jnp.ones(msg.shape[0], dtype=msg.dtype), seg, num_segments=N * T)
        msg = msg / counts[seg][:, None]
        agg = jax.ops.segment_sum(msg, dst, num_segments=N)
        hN = jnp.einsum('nd,tdf->tnf', feats, W_node) + b_node[:, None, :]
        out = hN[ntypes, jnp.arange(N)] + agg
        return jax.nn.relu(out)
    h = jnp.maximum(_layernorm(x, axis=-1), 0.0)
    x = x + _L0_gnn_ref(h, L0_gnn_W_edge, L0_gnn_b_edge, L0_gnn_W_node, L0_gnn_b_node, src, dst, node_type_8, edge_type_16)
    return x

_drawn_inputs = setup_inputs


def setup_inputs(seed=0):
    import zlib

    import numpy as np

    out = dict(_drawn_inputs(seed))
    spreads = {}
    factors = {'L0_gnn_b_node': 7.548}
    for name, (base, spread) in spreads.items():
        noise = np.random.default_rng([zlib.crc32(name.encode()), seed]).standard_normal(out[name].shape)
        drawn = base * np.exp(spread * noise) if base else spread * noise
        out[name] = jnp.asarray(drawn.astype(out[name].dtype))
    for name, factor in factors.items():
        out[name] = (out[name] * factor).astype(out[name].dtype)
    return out
```

```python
import concourse.bass as bass
from concourse import mybir
from contextlib import ExitStack

F32, F16, I32 = mybir.dt.float32, mybir.dt.float16, mybir.dt.int32
ALU = mybir.AluOpType
ACT = mybir.ActivationFunctionType
AX = mybir.AxisListType


def gnn_layer(nc, x, src, dst, etype, ntype, w_edge, b_edge, w_node, b_node, out):
    N, D = x.shape
    E = src.shape[0]
    R = w_edge.shape[0]
    K = w_node.shape[0]
    P = 128
    NB = (N + P - 1) // P
    NLAST = N - (NB - 1) * P
    NT = (E + P - 1) // P
    NTF = E // P
    ELAST = E - NTF * P
    CH = (NT + P - 1) // P
    TC = CH * P
    PAIRS = (NT + 1) // 2
    W = 24
    RING = 4 * P
    PPB = 8
    LATE = 3
    BODY = 4 * PPB
    ITERS = (PAIRS - LATE) // BODY
    assert PAIRS - LATE - ITERS * BODY == 1 and NB == 4 * ITERS + 1 and R * W <= 512
    AHEAD = 128
    H_SCALE = 4096.0
    PADTYPE = 64
    PER = BODY + 2
    CB = 14
    CITERS = PAIRS // (2 * CB)
    assert CITERS * 2 * CB == PAIRS and CB * W <= 512

    h_table = nc.dram_tensor("h_table", (NB * P, 2 * D), F16, kind="Internal").ap()
    rc_table = nc.dram_tensor("rc_table", (NB, R, P), F32, kind="Internal").ap()

    ctx = ExitStack()
    with ctx:
        def sb(name, shape, dt):
            return ctx.enter_context(nc.sbuf_tensor(name, shape, dt))

        def ps(name, shape, dt=F32):
            return ctx.enter_context(nc.psum_tensor(name, shape, dt))

        def sem(name):
            return ctx.enter_context(nc.semaphore(name))

        xs = sb("xs", [P, NB, D], F32)
        hh = sb("hh", [P, NB, 2 * D], F16)
        union_a = sb("union_a", [P, 2 * R * P], F32)
        ynorm = union_a[:, 0:NB * D].rearrange("p (b d) -> p b d", d=D)
        Sn = union_a[:, :].rearrange("p (q t n) -> p q t n", q=2, t=R)
        union_b = sb("union_b", [P, 2 * R * P], F32)
        MROWS = 3 * CH + 1
        meta_i = union_b[:, 0:MROWS * P].bitcast(I32).rearrange("p (c e) -> p c e", e=P)
        meta_f = union_b[:, MROWS * P:2 * MROWS * P].rearrange("p (c e) -> p c e", e=P)
        cnt = union_b[0:R, 0:NB * P + W]
        rcb = union_b[:, :].rearrange("p (q t n) -> p q t n", q=2, t=R)
        stats = sb("stats", [P, NB, 6], F32)
        mv = sb("mv", [P, NB, 2], F32)
        rstd = sb("rstd", [P, 4, NB], F32)
        src_t = sb("src_t", [P, TC], I32)
        dst_t = sb("dst_t", [P, TC], F32)
        et_t = sb("et_t", [P, TC], F32)
        nt_t = sb("nt_t", [P, NB], F32)
        base_b = sb("base_b", [P, TC // 2], F32)
        rel = sb("rel", [P, TC], F32)
        seg = sb("seg", [P, TC], F32)
        nviol = sb("nviol", [P, 4], F32)
        base_i = sb("base_i", [1, TC // 2], I32)
        ring_i = sb("ring_i", [1, TC // 2], I32)
        flag = sb("flag", [1, 1], I32)
        pair16 = sb("pair16", [P, PAIRS], F32)
        iota = sb("iota", [P, R * P + 1], F16)
        iota_w = iota[:, 0:R * W]
        iota1 = iota[:, 1:R * P + 1]
        id32 = sb("id32", [P, P], F32)
        id16 = sb("id16", [P, P], F16)
        ones = sb("ones", [P, P], F32)
        kcol = sb("kcol", [P, 1], F32)
        wmask = sb("wmask", [P, NB, K], F32)
        w_all = sb("w_all", [P, R + K, D], F32)
        bias = sb("bias", [P, D], F32)
        bsel = sb("bsel", [P, NB * P], F32)
        S = sb("S", [P, R, RING + W], F32)
        G = sb("G", [P, 2 * (BODY + LATE), 2 * D], F16)
        src_s = sb("src_s", [P, 2 * BODY], I32)
        seg_s = sb("seg_s", [P, 2 * BODY], F32)
        oh = sb("oh", [P, 4, 2, R * W], F16)
        tcnt = sb("tcnt", [P, 2, 2 * CB, R], F16)
        ncnt = sb("ncnt", [P, 2, 2 * CB, W], F16)
        dg = sb("dg", [P, 2, K, P], F16)
        hN = sb("hN", [P, 2, K, P], F32)
        viol = hN[:, 0, 0:TC // P, :].rearrange("p k n -> p (k n)")
        viol2 = hN[:, 1, 0:2, 0:P].rearrange("p k n -> p (k n)")[:, 0:PAIRS]
        bs = sb("bs", [64, 2, P], F32)
        os_ = sb("os", [P, 2, D], F32)
        nt_row = G[:, :, :].rearrange("p s d -> p (s d)").bitcast(I32)[:, 0:NB * P]
        goh = G[:, 8:8 + R * P // (2 * D), :].rearrange("p s d -> p (s d)")
        grc = sb("grc", [R, P], F32)
        gn = sb("gn", [P, P], F16)
        gt = sb("gt", [P, R], F16)
        zcol = sb("zcol", [P, 1], F32)
        zeros3 = zcol[:, :].unsqueeze(2).to_broadcast([P, R, P])
        gcol = sb("gcol", [P, 6], F32)
        bbase = sb("bbase", [P, 2], F32)

        acc = [ps(f"acc{q}", [P, 512]) for q in range(4)]
        misc = ps("misc", [P, 512])
        node_ps = ps("node_ps", [P, K, P])
        out_ps = ps("out_ps", [P, P])

        xpad_set = sem("xpad_set")
        x_in = [sem(f"x_in{c}") for c in range(5)]
        meta_in = sem("meta_in")
        w_in = sem("w_in")
        ntrow_in = sem("ntrow_in")
        consts = sem("consts")
        vstep = sem("vstep")
        meta_cast = sem("meta_cast")
        meta_tr = sem("meta_tr")
        dst_out = sem("dst_out")
        base_bc = sem("base_bc")
        var_ready = sem("var_ready")
        std_ready = sem("std_ready")
        h_ready = sem("h_ready")
        h_stored = sem("h_stored")
        src_ready = sem("src_ready")
        seg_ready = sem("seg_ready")
        viol_ready = sem("viol_ready")
        viol_sum = sem("viol_sum")
        flag_ready = sem("flag_ready")
        zeroed_s = sem("zeroed_s")
        mask_ready = sem("mask_ready")
        cvec = sem("cvec")
        c_oh = sem("c_oh")
        c_mm = sem("c_mm")
        c_acc = sem("c_acc")
        rc_ready = sem("rc_ready")
        rc_stored = sem("rc_stored")
        issuing = sem("issuing")
        gathered = [sem(f"gathered{u}") for u in range(BODY)]
        gathered_p = [sem(f"gathered_p{u}") for u in range(LATE)]
        staged = sem("staged")
        oh_ready = sem("oh_ready")
        pair_mm = sem("pair_mm")
        s_add = sem("s_add")
        rc_in = [sem("rc_in0"), sem("rc_in1")]
        scaled = sem("scaled")
        zeroed = sem("zeroed")
        dg_ready = sem("dg_ready")
        node_mm = sem("node_mm")
        hn_ready = sem("hn_ready")
        out_mm = sem("out_mm")
        fin = sem("fin")
        os_free = sem("os_free")
        stored = [sem("stored0"), sem("stored1")]
        g_src = sem("g_src")
        g_rows = sem("g_rows")
        g_vec = sem("g_vec")
        g_oh = sem("g_oh")
        g_mm = sem("g_mm")
        g_blk = sem("g_blk")
        g_rc = sem("g_rc")
        g_rcst = sem("g_rcst")

        FLAG_MAX = 1 << 20

        def sp_load_rc(sp, b, p):
            sp.wait_ge(scaled, b + 1)
            sp.dma_start(rcb[:, p, :, :].rearrange("p t n -> p (t n)"),
                         rc_table[bass.ds(b, 1)].rearrange("o t n -> o (t n)").to_broadcast([P, R * P])
                         ).then_inc(rc_in[p], 16)

        def sp_store(sp, b, p, use, rows=P):
            sp.wait_ge(fin, b + 3)
            sp.dma_start(out[bass.ds(b * P, rows), :], os_[0:rows, p, :]).then_inc(stored[p], 16)
            sp.wait_ge(stored[p], (use + 1) * 16)
            sp.sem_inc(os_free, 1)

        def act_node(act, b, p):
            act.wait_ge(node_mm, b + 1)
            for k in range(K):
                last = nc.scalar.activation(dg[:, p, k, :], id16[:, :], ACT.Copy,
                                            scale=wmask[:, bass.ds(b, 1), k])
            last.then_inc(dg_ready, 1)

        def act_node_out(act, b, p):
            act.wait_ge(node_mm, b + 3)
            act.wait_ge(out_mm, b + 1)
            nc.scalar.activation(bs[0:40, p, :], bsel[0:40, bass.ds(b * P, P)], ACT.Copy)
            nc.scalar.activation(hN[:, p, :, :], node_ps[:, :, :], ACT.Copy,
                                 scale=1.0 / H_SCALE).then_inc(hn_ready, 1)

        def act_zero(act, b, r):
            act.wait_ge(scaled, b + 3)
            nc.scalar.activation(S[:, :, r * P:(r + 1) * P], zeros3, ACT.Copy).then_inc(zeroed, 1)

        def pe_node(pe, b, p):
            pe.wait_ge(dg_ready, b + 1)
            pe.wait_ge(hn_ready, b + 1)
            for half in range(2):
                kk = slice(half * K // 2, (half + 1) * K // 2)
                for part in range(2):
                    last = nc.tensor.matmul(node_ps[:, kk, :],
                                            hh[:, bass.ds(b, 1), part * D:(part + 1) * D].rearrange("p o d -> p (o d)"),
                                            dg[:, p, kk, :], start=(part == 0), stop=(part == 1))
            last.then_inc(node_mm, 1)

        def pe_out(pe, b, p):
            pe.wait_ge(hn_ready, b + 2)
            pe.wait_ge(fin, b + 2)
            for k in range(K):
                nc.tensor.matmul(out_ps[:, :], hN[:, p, k, :], w_all[:, R + k, :],
                                 start=(k == 0), stop=False)
            nc.tensor.matmul(out_ps[:, :], bs[0:40, p, :], bias[0:40, :], start=False, stop=False)
            pe.wait_ge(scaled, b + 3)
            for t in range(R):
                last = nc.tensor.matmul(out_ps[:, :], Sn[:, p, t, :], w_all[:, t, :],
                                        start=False, stop=(t == R - 1))
            last.then_inc(out_mm, 1)

        def dve_scale(dve, b, p, r, use):
            dve.wait_ge(rc_in[p], (use + 1) * 16)
            dve.wait_ge(out_mm, b + 1)
            dve.wait_ge(zeroed, b + 1)
            nc.vector.tensor_tensor(Sn[:, p, :, :], S[:, :, r * P:(r + 1) * P], rcb[:, p, :, :],
                                    ALU.mult).then_inc(scaled, 1)

        def dve_finish(dve, b, p):
            dve.wait_ge(out_mm, b + 3)
            dve.wait_ge(os_free, b + 1)
            nc.vector.scalar_tensor_tensor(os_[:, p, :], out_ps[:, :], 0.0,
                                           xs[:, bass.ds(b, 1), :].rearrange("p o d -> p (o d)"),
                                           ALU.max, ALU.add).then_inc(fin, 1)


        def gather(pool, slot, index, done):
            nc.gpsimd.indirect_dma_start(
                out=G[:, slot, :], out_offset=None, in_=h_table[:, :],
                in_offset=bass.IndirectOffsetOnAxis(ap=index, axis=0)).then_inc(done, 16)

        block = ctx.enter_context(nc.Block())

        @block.sync
        def _(sp):
            sp.wait_ge(xpad_set, 1)
            for c in range(5):
                full = min(5, NB - 1 - 5 * c)
                sp.dma_start(xs[:, 5 * c:5 * c + full, :],
                             x[5 * c * P:(5 * c + full) * P, :].rearrange("(b p) d -> p b d", p=P)
                             ).then_inc(x_in[c], 16)
            sp.dma_start(xs[0:NLAST, NB - 1, :], x[(NB - 1) * P:N, :]).then_inc(x_in[4], 16)
            sp.dma_start(w_all[:, 0:R, :], w_edge.rearrange("t d f -> d t f")).then_inc(w_in, 16)
            sp.dma_start(w_all[:, R:R + K, :], w_node.rearrange("t d f -> d t f")).then_inc(w_in, 16)
            sp.wait_ge(consts, 2)
            sp.dma_start(bias[0:R, :], b_edge[:, :]).then_inc(w_in, 16)
            sp.dma_start(bias[32:32 + K, :], b_node[:, :]).then_inc(w_in, 16)
            for c in range(5):
                sp.wait_ge(h_ready, c + 1)
                sp.dma_start(h_table[5 * c * P:5 * (c + 1) * P, :].rearrange("(b p) d -> p b d", p=P),
                             hh[:, 5 * c:5 * (c + 1), :]).then_inc(h_stored, 16)

            sp.wait_ge(flag_ready, 1)
            bad = sp.value_load(flag[0:1, 0:1], min_val=0, max_val=FLAG_MAX)
            with sp.If(bad < 1):
                sp.wait_ge(rc_ready, 1)
                sp.dma_start(rc_table.rearrange("b t n -> t b n"),
                             cnt[:, 0:NB * P].rearrange("t (b n) -> t b n", n=P)).then_inc(rc_stored, 16)
                sp.wait_ge(rc_stored, 16)
                with sp.Fori(0, ITERS) as i:
                    for g in range(4):
                        sp_load_rc(sp, 4 * i + g, g % 2)
                        if g > 0:
                            sp_store(sp, 4 * i + g - 1, (g - 1) % 2, 2 * i + (g - 1) // 2)
                    sp_store(sp, 4 * i + 3, 1, 2 * i + 1)
                sp_load_rc(sp, NB - 1, 0)
                sp_store(sp, NB - 1, 0, (NB - 1) // 2, NLAST)
            with sp.Else():
                def one(b, p, use, rows=P):
                    sp.wait_ge(g_rc, b + 1)
                    sp.dma_start(rc_table[bass.ds(b, 1)].rearrange("o t n -> (o t) n"),
                                 grc[:, :]).then_inc(g_rcst, 16)
                    sp.wait_ge(g_rcst, (b + 1) * 16)
                    sp_load_rc(sp, b, p)
                    sp_store(sp, b, p, use, rows)
                with sp.Fori(0, (NB - 1) // 2) as i:
                    one(2 * i, 0, i)
                    one(2 * i + 1, 1, i)
                one(NB - 1, 0, (NB - 1) // 2, NLAST)
            sp.wait_ge(stored[0], 16 * ((NB + 1) // 2))
            sp.wait_ge(stored[1], 16 * (NB // 2))

        @block.gpsimd
        def _(pool):
            nc.gpsimd.memset(ones[:, :], 1.0)
            nc.gpsimd.memset(zcol[:, :], 0.0)
            nc.gpsimd.memset(id32[:, :], 0.0).then_inc(consts, 1)
            nc.gpsimd.memset(bias[:, :], 0.0).then_inc(consts, 1)
            pool.wait_ge(consts, 2)
            nc.gpsimd.affine_select(out=id32[:, :], in_=id32[:, :], compare_op=ALU.not_equal, fill=1.0,
                                    base=0, pattern=[[-1, P]], channel_multiplier=1).then_inc(consts, 1)
            pool.wait_ge(consts, 3)
            nc.gpsimd.tensor_copy(id16[:, :], id32[:, :]).then_inc(consts, 1)
            with nc.allow_low_precision(reason="integers up to 2048 are exact in float16"):
                nc.gpsimd.iota(iota[:, :], pattern=[[1, R * P + 1]], base=0, channel_multiplier=0,
                               allow_small_or_imprecise_dtypes=True)
            nc.gpsimd.iota(pair16[:, :], pattern=[[16, PAIRS]], base=0, channel_multiplier=0,
                           allow_small_or_imprecise_dtypes=True).then_inc(consts, 1)
            pool.wait_ge(consts, 5)
            nc.gpsimd.iota(kcol[32:64, :], pattern=[[0, 1]], base=0, channel_multiplier=1,
                           allow_small_or_imprecise_dtypes=True).then_inc(consts, 1)
            pool.wait_ge(consts, 6)
            nc.gpsimd.memset(S[:, :, :], 0.0).then_inc(zeroed_s, 1)
            nc.gpsimd.memset(bsel[0:64, :], 0.0).then_inc(zeroed_s, 1)

            pool.wait_ge(src_ready, 1)
            pool.wait_ge(h_stored, 16 * 5)
            pool.wait_ge(flag_ready, 1)
            bad = pool.value_load(flag[0:1, 0:1], min_val=0, max_val=FLAG_MAX)
            with pool.If(bad < 1):
                def may_issue():
                    pool.sem_inc(issuing, 1)
                for j in range(LATE):
                    for a in range(2):
                        gather(pool, 2 * (BODY + j) + a, src_t[:, 2 * j + a:2 * j + a + 1], gathered_p[j])
                with pool.Fori(0, ITERS) as i:
                    for u in range(BODY):
                        if u % PPB == 0:
                            pool.wait_ge(pair_mm, LATE + BODY * i + u + PPB)
                        if u % (BODY // 2) == 0:
                            pool.wait_ge(staged, 2 * i + u // (BODY // 2) + 1)
                        if u % PPB == 0:
                            may_issue()
                        for a in range(2):
                            gather(pool, 2 * u + a, src_s[:, 2 * u + a:2 * u + a + 1], gathered[u])
                pool.wait_ge(pair_mm, LATE + BODY * ITERS + PPB)
                j = PAIRS - 1
                for a in range(2):
                    gather(pool, a, src_t[:, 2 * j + a:2 * j + a + 1], gathered[0])
            with pool.Else():
                with pool.Fori(0, NB * NT) as n:
                    pool.wait_ge(g_src, n + 1)
                    pool.sem_inc(issuing, 1)
                    gather(pool, 0, src_s[:, 0:1], g_rows)
                    pool.wait_ge(g_rows, (n + 1) * 16)

        @block.scalar
        def _(act):
            act.wait_ge(xpad_set, 1)
            row = 0
            for arr in (src, dst, etype):
                act.dma_start(meta_i[:, row:row + CH - 1, :],
                              arr[0:(CH - 1) * P * P].rearrange("(c p e) -> p c e", p=P, e=P)
                              ).then_inc(meta_in, 16)
                full = NTF - (CH - 1) * P
                act.dma_start(meta_i[0:full, row + CH - 1, :],
                              arr[(CH - 1) * P * P:NTF * P].rearrange("(p e) -> p e", e=P)
                              ).then_inc(meta_in, 16)
                act.dma_start(meta_i[full:full + 1, row + CH - 1, 0:ELAST],
                              arr[NTF * P:E].rearrange("(o e) -> o e", o=1)).then_inc(meta_in, 16)
                row += CH
            act.dma_start(meta_i[0:NB - 1, row, :],
                          ntype[0:(NB - 1) * P].rearrange("(p e) -> p e", e=P)).then_inc(meta_in, 16)
            act.dma_start(meta_i[NB - 1:NB, row, 0:NLAST],
                          ntype[(NB - 1) * P:N].rearrange("(o e) -> o e", o=1)).then_inc(meta_in, 16)
            act.dma_start(nt_row[32:32 + K, 0:N],
                          ntype.rearrange("(o n) -> o n", o=1).to_broadcast([K, N])).then_inc(ntrow_in, 16)
            act.wait_ge(meta_tr, 1)
            nc.scalar.activation(src_t[:, :], acc[0][:, 0:TC], ACT.Copy).then_inc(src_ready, 1)
            act.wait_ge(var_ready, 1)
            nc.scalar.activation(rstd[:, 1, :], rstd[:, 0, :], ACT.Sqrt).then_inc(std_ready, 1)
            act.wait_ge(mask_ready, 1)
            act.wait_ge(consts, 6)
            act.wait_ge(src_ready, 1)
            for s in (zeroed, hn_ready):
                act.sem_inc(s, 1)
            act.wait_ge(flag_ready, 1)
            bad = act.value_load(flag[0:1, 0:1], min_val=0, max_val=FLAG_MAX)
            with act.If(bad < 1):
                H = BODY // 2

                def stage(i, half):
                    c0 = 2 * LATE + 2 * BODY * i + 2 * H * half
                    nc.scalar.activation(src_s[:, 2 * H * half:2 * H * (half + 1)],
                                         src_t[:, bass.ds(c0, 2 * H)], ACT.Copy)
                    nc.scalar.activation(seg_s[:, 2 * H * half:2 * H * (half + 1)],
                                         seg[:, bass.ds(c0, 2 * H)], ACT.Copy).then_inc(staged, 1)
                stage(0, 0)
                stage(0, 1)
                act_node(act, 0, 0)
                act.wait_ge(rc_ready, 1)
                with act.Fori(0, ITERS) as i:
                    for g in range(4):
                        b = 4 * i + g
                        act_node_out(act, b, g % 2)
                        act_node(act, b + 1, (g + 1) % 2)
                        if g % 2 == 1:
                            act.wait_ge(pair_mm, BODY + LATE + BODY * i + (g + 1) * PPB)
                            stage(i + 1, g // 2)
                        act_zero(act, b, g)
                act_node_out(act, NB - 1, 0)
            with act.Else():
                def sweep(b):
                    with act.Fori(0, NT) as t:
                        n = b * NT + t
                        act.wait_ge(g_mm, n + 1)
                        nc.scalar.activation(src_s[:, 0:1], src_t[:, bass.ds(t, 1)],
                                             ACT.Copy).then_inc(g_src, 1)

                def one(b, p):
                    sweep(b)
                    act_node(act, b, p)
                    act.wait_ge(g_rc, b + 1)
                    act_node_out(act, b, p)
                    act_zero(act, b, p)
                with act.Fori(0, (NB - 1) // 2) as i:
                    one(2 * i, 0)
                    one(2 * i + 1, 1)
                one(NB - 1, 0)

        @block.tensor
        def _(pe):
            pe.wait_ge(consts, 6)
            pe.wait_ge(meta_cast, 1)
            for a in range(3):
                for c in range(CH):
                    last = nc.tensor.transpose(acc[a][:, c * P:(c + 1) * P], meta_f[:, a * CH + c, :], id32[:, :])
                last.then_inc(meta_tr, 1)
            nc.tensor.transpose(misc[:, 0:P], meta_f[:, 3 * CH, :], id32[:, :]).then_inc(meta_tr, 1)
            pe.wait_ge(dst_out, 1)
            nc.tensor.matmul(acc[3][:, 0:TC // 2], ones[0:1, :], dst_t[0:1, 0:TC:2],
                             start=True, stop=True).then_inc(base_bc, 1)
            pe.wait_ge(viol_ready, 1)
            nc.tensor.matmul(misc[0:1, 256:257], ones[:, 0:1], nviol[:, 2:3],
                             start=True, stop=True).then_inc(viol_sum, 1)
            pe.wait_ge(w_in, 64)
            pe.wait_ge(h_ready, 5)
            pe.wait_ge(src_ready, 1)
            for s in (node_mm, out_mm):
                pe.sem_inc(s, 2)
            pe.sem_inc(pair_mm, BODY)
            for s in (c_mm, g_mm):
                pe.sem_inc(s, 1)
            pe.wait_ge(flag_ready, 1)
            bad = pe.value_load(flag[0:1, 0:1], min_val=0, max_val=FLAG_MAX)
            with pe.If(bad < 1):
                with pe.Fori(0, CITERS) as i:
                    for q in range(2):
                        pe.wait_ge(c_oh, 2 * i + q + 1)
                        pe.wait_ge(c_acc, (2 * i + q) * CB + 1)
                        for v in range(CB):
                            for a in range(2):
                                last = nc.tensor.matmul(acc[2 + q][0:R, v * W:(v + 1) * W],
                                                        tcnt[:, q, 2 * v + a, :], ncnt[:, q, 2 * v + a, :],
                                                        start=(a == 0), stop=(a == 1))
                        last.then_inc(c_mm, 1)

                def sums(pair, bank, g_slot, o, got, got_value, added):
                    pe.wait_ge(got, got_value)
                    pe.wait_ge(oh_ready, pair + 1)
                    pe.wait_ge(s_add, added)
                    for a in range(2):
                        for part in range(2):
                            last = nc.tensor.matmul(acc[bank][:, 0:R * W],
                                                    G[:, 2 * g_slot + a, part * D:(part + 1) * D],
                                                    oh[:, o, a, :], start=(a + part == 0),
                                                    stop=(a + part == 2))
                    last.then_inc(pair_mm, 1)
                for j in range(LATE):
                    sums(j, j % 2, BODY + j, (j - LATE) % 4, gathered_p[j], 32, max(0, j - 1))
                pe_node(pe, 0, 0)
                with pe.Fori(0, ITERS) as i:
                    for u in range(BODY):
                        sums(i * BODY + LATE + u, (u + LATE) % 2, u, u % 4, gathered[u], 32 * i + 32,
                             LATE + i * PER + max(0, u - 1))
                        if u % PPB == 5:
                            pe_node(pe, 4 * i + u // PPB + 1, (u // PPB + 1) % 2)
                        if u % PPB == 2 and u > PPB:
                            pe_out(pe, 4 * i + u // PPB - 1, (u // PPB - 1) % 2)
                    pe_out(pe, 4 * i + 3, 1)
                sums(PAIRS - 1, (PAIRS - 1) % 2, 0, 0, gathered[0], 32 * ITERS + 32,
                     LATE + ITERS * PER)
                pe_out(pe, NB - 1, 0)
            with pe.Else():
                def tile(n, first, last_tile):
                    pe.wait_ge(g_rows, (n + 1) * 16)
                    pe.wait_ge(g_oh, n + 1)
                    for q in range(4):
                        for part in range(2):
                            nc.tensor.matmul(acc[q][:, :], G[:, 0, part * D:(part + 1) * D],
                                             goh[:, q * 512:(q + 1) * 512],
                                             start=first and part == 0, stop=last_tile and part == 1)
                    nc.tensor.matmul(misc[0:R, 0:P], gt[:, :], gn[:, :],
                                     start=first, stop=last_tile).then_inc(g_mm, 1)

                def one(b, p):
                    pe.wait_ge(g_blk, b + 1)
                    tile(b * NT, True, False)
                    with pe.Fori(1, NT - 1) as t:
                        tile(b * NT + t, False, False)
                    tile(b * NT + NT - 1, False, True)
                    pe_node(pe, b, p)
                    pe_out(pe, b, p)
                with pe.Fori(0, (NB - 1) // 2) as i:
                    one(2 * i, 0)
                    one(2 * i + 1, 1)
                one(NB - 1, 0)

        @block.vector
        def _(dve):
            steps = [0]

            def own(ins):
                ins.then_inc(vstep, 1)
                steps[0] += 1

            def settle():
                dve.wait_ge(vstep, steps[0])

            nc.vector.memset(xs[:, NB - 1, :], 0.0)
            for row, value in ((CH - 1, 0), (2 * CH - 1, N - 1), (3 * CH - 1, PADTYPE), (3 * CH, PADTYPE)):
                last = nc.vector.memset(meta_i[:, row, :], value)
            last.then_inc(xpad_set, 1)
            own(nc.vector.memset(nt_row[32:64, N:NB * P], PADTYPE))
            for c in range(5):
                dve.wait_ge(x_in[c], 32 if c == 4 else 16)
                for b in range(5 * c, 5 * c + 5):
                    own(nc.vector.bn_stats(stats[:, b, :], xs[:, b, :]))
            settle()
            for b in range(NB):
                own(nc.vector.bn_aggr(mv[:, b, :], stats[:, b, :]))
            settle()
            nc.vector.tensor_scalar(rstd[:, 0, :], mv[:, :, 1], 1e-5, None, ALU.add).then_inc(var_ready, 1)
            dve.wait_ge(meta_in, 16 * 11)
            nc.vector.tensor_copy(meta_f[:, :, :], meta_i[:, :, :]).then_inc(meta_cast, 1)
            dve.wait_ge(std_ready, 1)
            own(nc.vector.reciprocal(rstd[:, 2, :], rstd[:, 1, :]))
            settle()
            own(nc.vector.tensor_tensor(rstd[:, 3, :], rstd[:, 2, :], rstd[:, 2, :], ALU.mult))
            settle()
            own(nc.vector.tensor_tensor(rstd[:, 3, :], rstd[:, 3, :], rstd[:, 0, :], ALU.mult))
            settle()
            own(nc.vector.tensor_scalar(rstd[:, 3, :], rstd[:, 3, :], -0.5 * H_SCALE, 1.5 * H_SCALE,
                                        ALU.mult, ALU.add))
            settle()
            own(nc.vector.tensor_tensor(rstd[:, 3, :], rstd[:, 3, :], rstd[:, 2, :], ALU.mult))
            settle()
            for c in range(5):
                bb = slice(5 * c, 5 * c + 5)
                for b in range(5 * c, 5 * c + 5):
                    own(nc.vector.tensor_scalar(ynorm[:, b, :], xs[:, b, :], mv[:, b, 0:1], rstd[:, 3, b:b + 1],
                                                ALU.subtract, ALU.mult))
                settle()
                own(nc.vector.tensor_scalar(hh[:, bb, 0:D], ynorm[:, bb, :], 0.0, None, ALU.max))
                settle()
                nc.vector.scalar_tensor_tensor(hh[:, bb, D:2 * D], ynorm[:, bb, :], 0.0, hh[:, bb, 0:D],
                                               ALU.max, ALU.subtract).then_inc(h_ready, 1)
            dve.wait_ge(meta_tr, 4)
            nc.vector.tensor_copy(dst_t[:, :], acc[1][:, :]).then_inc(dst_out, 1)
            own(nc.vector.tensor_copy(et_t[:, :], acc[2][:, :]))
            own(nc.vector.tensor_copy(nt_t[:, :], misc[:, 0:NB]))
            dve.wait_ge(base_bc, 1)
            own(nc.vector.tensor_copy(base_b[:, :], acc[3][:, 0:TC // 2]))
            dve.wait_ge(dst_out, 1)
            own(nc.vector.tensor_copy(base_i[:, :], dst_t[0:1, 0:TC:2]))
            settle()
            own(nc.vector.tensor_tensor(rel[:, :].rearrange("p (j a) -> p j a", a=2),
                                        dst_t[:, :].rearrange("p (j a) -> p j a", a=2),
                                        base_b[:, :].unsqueeze(2).to_broadcast([P, TC // 2, 2]), ALU.subtract))
            own(nc.vector.tensor_scalar(ring_i[:, :], base_i[:, :], RING - 1, None, ALU.bitwise_and))
            settle()
            own(nc.vector.scalar_tensor_tensor(seg[:, :], et_t[:, :], float(W), rel[:, :], ALU.mult, ALU.add))
            own(nc.vector.tensor_scalar(viol[:, 0:2 * PAIRS], rel[:, 0:2 * PAIRS], 0.0, None, ALU.is_lt))
            dve.wait_ge(consts, 6)
            own(nc.vector.tensor_tensor(base_b[:, 0:PAIRS], base_b[:, 0:PAIRS], pair16[:, :], ALU.subtract))
            settle()
            own(nc.vector.scalar_tensor_tensor(viol[:, 0:2 * PAIRS], rel[:, 0:2 * PAIRS], float(W - 1),
                                               viol[:, 0:2 * PAIRS], ALU.is_gt, ALU.add))
            own(nc.vector.tensor_scalar(viol2[:, :], base_b[:, 0:PAIRS], -16.0 * LATE, None, ALU.is_lt))
            settle()
            own(nc.vector.scalar_tensor_tensor(viol2[:, :], base_b[:, 0:PAIRS], float(AHEAD), viol2[:, :],
                                               ALU.is_gt, ALU.add))
            own(nc.vector.tensor_reduce(nviol[:, 0:1], viol[:, 0:2 * PAIRS], AX.X, ALU.add))
            settle()
            own(nc.vector.tensor_reduce(nviol[:, 1:2], viol2[:, :], AX.X, ALU.add))
            settle()
            nc.vector.tensor_tensor(nviol[:, 2:3], nviol[:, 0:1], nviol[:, 1:2], ALU.add).then_inc(viol_ready, 1)
            own(nc.vector.tensor_tensor(wmask[:, :, :], nt_t[:, :].unsqueeze(2).to_broadcast([P, NB, K]),
                                        iota_w[:, 0:K].unsqueeze(1).to_broadcast([P, NB, K]), ALU.is_equal))
            dve.wait_ge(ntrow_in, 16)
            dve.wait_ge(zeroed_s, 2)
            own(nc.vector.tensor_scalar(bsel[32:32 + K, :], nt_row[32:32 + K, :], kcol[32:32 + K, :], None,
                                        ALU.is_equal))
            settle()
            dve.sem_inc(mask_ready, 1)
            for s in (scaled, fin, os_free):
                dve.sem_inc(s, 2)
            for s in (c_acc, g_blk):
                dve.sem_inc(s, 1)
            dve.wait_ge(viol_sum, 1)
            nc.vector.tensor_copy(flag[:, :], misc[0:1, 256:257]).then_inc(flag_ready, 1)
            dve.wait_ge(flag_ready, 1)
            bad = dve.value_load(flag[0:1, 0:1], min_val=0, max_val=FLAG_MAX)

            def rc_of(rc, ind, count, steps_before, done):
                nc.vector.tensor_scalar(ind, count, 1.0, None, ALU.min).then_inc(cvec, 1)
                nc.vector.tensor_scalar(rc, count, 1.0, H_SCALE, ALU.max, ALU.mult).then_inc(cvec, 1)
                dve.wait_ge(cvec, steps_before + 2)
                nc.vector.reciprocal(rc, rc).then_inc(done, 1)

            with dve.If(bad < 1):
                def count_oh(batch, q):
                    c0 = batch * 2 * CB
                    nc.vector.tensor_tensor(tcnt[:, q, :, :],
                                            et_t[:, bass.ds(c0, 2 * CB)].unsqueeze(2).to_broadcast([P, 2 * CB, R]),
                                            iota_w[:, 0:R].unsqueeze(1).to_broadcast([P, 2 * CB, R]), ALU.is_equal)
                    nc.vector.tensor_tensor(ncnt[:, q, :, :],
                                            rel[:, bass.ds(c0, 2 * CB)].unsqueeze(2).to_broadcast([P, 2 * CB, W]),
                                            iota_w[:, 0:W].unsqueeze(1).to_broadcast([P, 2 * CB, W]),
                                            ALU.is_equal).then_inc(c_oh, 1)

                def windows(row, c0, n):
                    got = []
                    for v in range(0, n, 4):
                        m = min(4, n - v)
                        got += nc.values_load_multi_w_load_instructions(
                            row[0:1, bass.ds(c0 + v, m)], engines=[mybir.EngineType.DVE], min_val=0,
                            max_val=(RING - 1 if row is ring_i else N - 1),
                            skip_runtime_bounds_check_because="dst is a node; the path's test bounds it")[1]
                    return got

                dve.wait_ge(meta_tr, 4)
                nc.vector.memset(cnt[:, :], 0.0).then_inc(cvec, 1)
                count_oh(0, 0)
                dve.wait_ge(cvec, 1)
                with dve.Fori(0, CITERS) as i:
                    for q in range(2):
                        batch = 2 * i + q
                        dve.wait_ge(c_mm, batch + 1)
                        count_oh(batch + 1, 1 - q)
                        at = windows(base_i, batch * CB, CB)
                        dve.wait_ge(c_mm, batch + 2)
                        for v in range(CB):
                            dve.wait_ge(c_acc, batch * CB + v + 1)
                            span = cnt[:, bass.ds(at[v], W)]
                            nc.vector.tensor_tensor(span, span, acc[2 + q][0:R, v * W:(v + 1) * W],
                                                    ALU.add).then_inc(c_acc, 1)
                dve.wait_ge(c_acc, PAIRS + 1)
                rc_of(cnt[:, 0:NB * P], bsel[0:R, :], cnt[:, 0:NB * P], 1, rc_ready)

                def onehot(o, cols):
                    for a in range(2):
                        last = nc.vector.tensor_scalar(oh[:, o, a, :], iota_w[:, 0:R * W], cols[:, a:a + 1],
                                                       None, ALU.is_equal)
                    last.then_inc(oh_ready, 1)

                def add(pair, at, adds):
                    dve.wait_ge(pair_mm, BODY + pair + 1)
                    dve.wait_ge(s_add, adds)
                    span = S[:, :, bass.ds(at, W)]
                    nc.vector.tensor_tensor(span, span,
                                            acc_bank(pair_parity(pair)).rearrange("p (t n) -> p t n", n=W),
                                            ALU.add).then_inc(s_add, 1)
                parity = {}

                def pair_parity(pair):
                    return parity["now"]

                def acc_bank(q):
                    return acc[q][:, 0:R * W]

                onehot(1, seg[:, 0:2])
                onehot(2, seg[:, 2:4])
                onehot(3, seg[:, 4:6])
                at = windows(ring_i, 0, LATE)
                dve.wait_ge(staged, 1)
                for j in range(LATE):
                    parity["now"] = j % 2
                    add(j, at[j], j)
                    if j < 2:
                        onehot(j, seg_s[:, 2 * j:2 * j + 2])
                with dve.Fori(0, ITERS) as i:
                    n0 = LATE + i * PER
                    done = 0
                    for u in range(BODY):
                        pair = LATE + i * BODY + u
                        if u % 4 == 0:
                            at = windows(ring_i, LATE + i * BODY + u, 4)
                        if u == BODY // 2 - 2:
                            dve.wait_ge(staged, 2 * i + 2)
                        if u == BODY - 2:
                            dve.wait_ge(staged, 2 * i + 3)
                        w = (u + 2) % BODY
                        dve.wait_ge(pair_mm, BODY + pair - 1)
                        onehot(w % 4, seg_s[:, 2 * w:2 * w + 2])
                        parity["now"] = (u + LATE) % 2
                        add(pair, at[u % 4], n0 + done)
                        done += 1
                        g = u // PPB
                        if u == BODY - 1:
                            dve.wait_ge(zeroed, 4 * i + g + 1)
                            dve.wait_ge(s_add, n0 + done)
                            nc.vector.tensor_tensor(S[:, :, 0:W], S[:, :, 0:W], S[:, :, RING:RING + W],
                                                    ALU.add).then_inc(s_add, 1)
                            done += 1
                            dve.wait_ge(s_add, n0 + done)
                            nc.vector.memset(S[:, :, RING:RING + W], 0.0).then_inc(s_add, 1)
                            done += 1
                        if u % PPB == PPB - 1:
                            dve.wait_ge(s_add, n0 + done)
                            dve_scale(dve, 4 * i + g, g % 2, g, 2 * i + g // 2)
                        if u % PPB == 4 and u > PPB:
                            dve_finish(dve, 4 * i + g - 1, (g - 1) % 2)
                    assert done == PER
                    dve_finish(dve, 4 * i + 3, 1)
                at = windows(ring_i, PAIRS - 1, 1)
                parity["now"] = (PAIRS - 1) % 2
                add(PAIRS - 1, at[0], LATE + ITERS * PER)
                dve.wait_ge(s_add, LATE + ITERS * PER + 1)
                dve_scale(dve, NB - 1, 0, 0, (NB - 1) // 2)
                dve_finish(dve, NB - 1, 0)
            with dve.Else():
                nc.vector.memset(bbase[:, 0:1], 0.0).then_inc(g_vec, 1)
                GV = 6

                def tile(b, t):
                    n = b * NT + t
                    v0 = 1 + b + n * GV

                    def done(k):
                        dve.wait_ge(g_vec, v0 + k)
                    dve.wait_ge(g_mm, n + 1)
                    done(0)
                    d, v, lo, hi, col = (gcol[:, k:k + 1] for k in range(5))
                    nc.vector.tensor_tensor(v, dst_t[:, bass.ds(t, 1)], bbase[:, 0:1],
                                            ALU.subtract).then_inc(g_vec, 1)
                    done(1)
                    nc.vector.tensor_scalar(lo, v, 0.0, None, ALU.is_ge).then_inc(g_vec, 1)
                    nc.vector.tensor_scalar(hi, v, float(P), None, ALU.is_lt).then_inc(g_vec, 1)
                    nc.vector.scalar_tensor_tensor(col, et_t[:, bass.ds(t, 1)], float(P), v,
                                                   ALU.mult, ALU.add).then_inc(g_vec, 1)
                    done(4)
                    nc.vector.scalar_tensor_tensor(d, col, 1.0, lo, ALU.add, ALU.mult).then_inc(g_vec, 1)
                    done(5)
                    nc.vector.tensor_tensor(d, d, hi, ALU.mult).then_inc(g_vec, 1)
                    done(6)
                    nc.vector.tensor_scalar(goh[:, :], iota1[:, :], d, None, ALU.is_equal)
                    nc.vector.tensor_scalar(gn[:, :], iota_w[:, 0:P], v, None, ALU.is_equal)
                    nc.vector.tensor_scalar(gt[:, :], iota_w[:, 0:R], et_t[:, bass.ds(t, 1)], None,
                                            ALU.is_equal).then_inc(g_oh, 1)

                def one(b, p, use):
                    with dve.Fori(0, NT) as t:
                        tile(b, t)
                    dve.wait_ge(g_mm, (b + 1) * NT + 1)
                    dve.wait_ge(zeroed, b + 1)
                    for q in range(4):
                        nc.vector.tensor_copy(S[:, 4 * q:4 * q + 4, p * P:(p + 1) * P],
                                              acc[q][:, :].rearrange("p (t n) -> p t n", n=P)
                                              ).then_inc(s_add, 1)
                    rc_of(grc[:, :], bsel[0:R, bass.ds(b * P, P)], misc[0:R, 0:P], 2 * b, g_rc)
                    dve.wait_ge(s_add, 4 * b + 4)
                    nc.vector.tensor_scalar(bbase[:, 0:1], bbase[:, 0:1], float(P), None,
                                            ALU.add).then_inc(g_vec, 1)
                    dve.sem_inc(g_blk, 1)
                    dve_scale(dve, b, p, p, use)
                    dve_finish(dve, b, p)
                with dve.Fori(0, (NB - 1) // 2) as i:
                    one(2 * i, 0, i)
                    one(2 * i + 1, 1, i)
                one(NB - 1, 0, (NB - 1) // 2)


_INS = ['x', 'src', 'dst', 'edge_type_16', 'node_type_8', 'L0_gnn_W_edge', 'L0_gnn_b_edge', 'L0_gnn_W_node',
        'L0_gnn_b_node']


def kernel(**inputs):
    import numpy as _np
    import concourse.bacc as _bacc
    from concourse import mybir as _mybir
    from concourse.bass_utils import run_bass_kernel_spmd as _run

    nc = _bacc.Bacc("TRN2", target_bir_lowering=False, num_devices=1)
    arrays, args = {}, []
    for name in _INS:
        a = _np.ascontiguousarray(inputs[name])
        arrays[f"in_{name}_dram"] = a
        args.append(nc.dram_tensor(f"in_{name}_dram", a.shape, _mybir.dt.from_np(a.dtype), kind="ExternalInput").ap())
    n, d = inputs['x'].shape
    args.append(nc.dram_tensor("out_0_dram", (n, d), _mybir.dt.float32, kind="ExternalOutput").ap())
    gnn_layer(nc, *args)
    r = _run(nc, [arrays], core_ids=[0])
    return r.results[0]["out_0_dram"]
```

```python
import concourse.bass as bass
from concourse import mybir
from contextlib import ExitStack

F32, F16, I32 = mybir.dt.float32, mybir.dt.float16, mybir.dt.int32
ALU = mybir.AluOpType
ACT = mybir.ActivationFunctionType
AX = mybir.AxisListType


def gnn_layer(nc, x, src, dst, etype, ntype, w_edge, b_edge, w_node, b_node, out):
    N, D = x.shape
    E = src.shape[0]
    R = w_edge.shape[0]
    K = w_node.shape[0]
    P = 128
    NB = (N + P - 1) // P
    SEG = 8
    NLAST = N - (NB - 1) * P
    NT = (E + P - 1) // P
    NTF = E // P
    ELAST = E - NTF * P
    CH = (NT + P - 1) // P
    TC = CH * P
    PAIRS = (NT + 1) // 2
    W = 24
    RING = 4 * P
    PPB = 8
    LATE = 3
    BODY = 4 * PPB
    ITERS = (PAIRS - LATE) // BODY
    assert PAIRS - LATE - ITERS * BODY == 1 and NB == 4 * ITERS + 1 and R * W <= 512
    AHEAD = 128
    H_SCALE = 4096.0
    PADTYPE = 64
    PER = BODY + 2
    QUADS = (NT + 3) // 4
    WQ = 44
    CB = 7
    CITERS = QUADS // (2 * CB)
    assert CITERS * 2 * CB == QUADS and 2 * QUADS == PAIRS and CB * WQ <= 512
    CN = NB * P + WQ
    RCW = NB * R * P // P

    h_table = nc.dram_tensor("h_table", (NB * P, 2 * D), F16, kind="Internal").ap()
    cnt_table = nc.dram_tensor("cnt_table", (NB, R, P), F32, kind="Internal").ap()
    rc_table = nc.dram_tensor("rc_table", (NB, R, P), F32, kind="Internal").ap()

    ctx = ExitStack()
    with ctx:
        def sb(name, shape, dt):
            return ctx.enter_context(nc.sbuf_tensor(name, shape, dt))

        def ps(name, shape, dt=F32):
            return ctx.enter_context(nc.psum_tensor(name, shape, dt))

        def sem(name):
            return ctx.enter_context(nc.semaphore(name))

        xs = sb("xs", [P, NB, D], F32)
        hh = sb("hh", [P, NB, 2 * D], F16)
        union_a = sb("union_a", [P, 2 * R * P], F32)
        ynorm = union_a[:, 0:NB * D].rearrange("p (b d) -> p b d", d=D)
        Sn = union_a[:, :].rearrange("p (q t n) -> p q t n", q=2, t=R)
        union_b = sb("union_b", [P, 2 * R * P], F32)
        MROWS = 3 * CH + 1
        meta_i = union_b[:, 0:MROWS * P].bitcast(I32).rearrange("p (c e) -> p c e", e=P)
        meta_f = union_b[:, MROWS * P:2 * MROWS * P].rearrange("p (c e) -> p c e", e=P)
        cnt_q = [union_b[0:R, 0:CN], union_a[0:R, 0:CN]]
        cnt = cnt_q[0]
        rc_w = union_a[:, CN:CN + RCW]
        rcb = union_b[:, :].rearrange("p (q t n) -> p q t n", q=2, t=R)
        stats = sb("stats", [P, NB, 6], F32)
        mv = sb("mv", [P, NB, 2], F32)
        rstd = sb("rstd", [P, 4, NB], F32)
        src_t = sb("src_t", [P, TC], I32)
        dst_t = sb("dst_t", [P, TC], F32)
        et_t = sb("et_t", [P, TC], F32)
        nt_t = sb("nt_t", [P, NB], F32)
        base_b = sb("base_b", [P, TC // 2], F32)
        rel = sb("rel", [P, TC], F32)
        seg = sb("seg", [P, TC], F32)
        relq = sb("relq", [P, 4 * QUADS], F16)
        et16 = sb("et16", [P, 4 * QUADS], F16)
        nviol = sb("nviol", [P, 1], F32)
        base_i = sb("base_i", [1, TC // 2], I32)
        ring_i = sb("ring_i", [1, TC // 2], I32)
        quad_i = sb("quad_i", [1, QUADS], I32)
        flag = sb("flag", [1, 1], I32)
        pair16 = sb("pair16", [P, PAIRS], F32)
        iota = sb("iota", [P, R * P + 1], F16)
        iota_w = iota[:, 0:R * W]
        iota1 = iota[:, 1:R * P + 1]
        id32 = sb("id32", [P, P], F32)
        id16 = sb("id16", [P, P], F16)
        ones = sb("ones", [P, P], F32)
        kcol = sb("kcol", [P, 1], F32)
        wmask = sb("wmask", [P, NB, K], F32)
        w_all = sb("w_all", [P, R + K, D], F32)
        bias = sb("bias", [P, D], F32)
        bsel = sb("bsel", [P, NB * P], F32)
        S = sb("S", [P, R, RING + W], F32)
        G = sb("G", [P, 2 * (BODY + LATE), 2 * D], F16)
        src_s = sb("src_s", [P, 2 * BODY], I32)
        seg_s = sb("seg_s", [P, 2 * BODY], F32)
        oh = sb("oh", [P, 4, 2, R * W], F16)
        tcnt = sb("tcnt", [P, 2, 4 * CB, R], F16)
        ncnt = sb("ncnt", [P, 2, 4 * CB, WQ], F16)
        dg = sb("dg", [P, 2, K, P], F16)
        hN = sb("hN", [P, 2, K, P], F32)
        viol = hN[:, :, :, :].rearrange("p q k n -> p (q k n)")
        bs = sb("bs", [64, 2, P], F32)
        os_ = sb("os", [P, 2, D], F32)
        nt_row = G[:, :, :].rearrange("p s d -> p (s d)").bitcast(I32)[:, 0:NB * P]
        goh = G[:, 8:8 + R * P // (2 * D), :].rearrange("p s d -> p (s d)")
        grc = sb("grc", [R, P], F32)
        gn = sb("gn", [P, P], F16)
        gt = sb("gt", [P, R], F16)
        zcol = sb("zcol", [P, 1], F32)
        zeros3 = zcol[:, :].unsqueeze(2).to_broadcast([P, R, P])
        gcol = sb("gcol", [P, 6], F32)
        bbase = sb("bbase", [P, 2], F32)

        acc = [ps(f"acc{q}", [P, 512]) for q in range(4)]
        misc = ps("misc", [P, 512])
        node_ps = ps("node_ps", [P, K, P])
        out_ps = ps("out_ps", [P, P])

        xpad_set = sem("xpad_set")
        x_in = [sem(f"x_in{c}") for c in range(5)]
        meta_in = sem("meta_in")
        w_in = sem("w_in")
        ntrow_in = sem("ntrow_in")
        consts = sem("consts")
        vstep = sem("vstep")
        rstd_ready = sem("rstd_ready")
        relu_done = sem("relu_done")
        meta_cast = sem("meta_cast")
        cnt_zeroed = sem("cnt_zeroed")
        cnt_ready = sem("cnt_ready")
        cnt_moved = sem("cnt_moved")
        ind_ready = sem("ind_ready")
        meta_tr = sem("meta_tr")
        dst_out = sem("dst_out")
        base_bc = sem("base_bc")
        var_ready = sem("var_ready")
        std_ready = sem("std_ready")
        h_ready = sem("h_ready")
        h_stored = sem("h_stored")
        src_ready = sem("src_ready")
        seg_ready = sem("seg_ready")
        viol_ready = sem("viol_ready")
        viol_sum = sem("viol_sum")
        flag_ready = sem("flag_ready")
        zeroed_s = sem("zeroed_s")
        mask_ready = sem("mask_ready")
        cvec = sem("cvec")
        c_oh = sem("c_oh")
        c_mm = sem("c_mm")
        c_out = sem("c_out")
        rc_ready = sem("rc_ready")
        rc_stored = sem("rc_stored")
        issuing = sem("issuing")
        gathered = [sem(f"gathered{u}") for u in range(BODY)]
        gathered_p = [sem(f"gathered_p{u}") for u in range(LATE)]
        staged = sem("staged")
        oh_ready = sem("oh_ready")
        pair_mm = sem("pair_mm")
        s_add = sem("s_add")
        rc_in = [sem("rc_in0"), sem("rc_in1")]
        scaled = sem("scaled")
        zeroed = sem("zeroed")
        dg_ready = sem("dg_ready")
        node_mm = sem("node_mm")
        hn_ready = sem("hn_ready")
        out_mm = sem("out_mm")
        fin = sem("fin")
        os_free = sem("os_free")
        stored = [sem("stored0"), sem("stored1")]
        g_src = sem("g_src")
        g_rows = [sem(f"g_rows{k}") for k in range(4)]
        g_vec = sem("g_vec")
        g_oh = sem("g_oh")
        g_mm = sem("g_mm")
        g_blk = sem("g_blk")
        g_rc = sem("g_rc")
        g_rcst = sem("g_rcst")

        FLAG_MAX = 1 << 20

        def sp_load_rc(sp, b, p):
            sp.wait_ge(scaled, b + 1)
            sp.dma_start(rcb[:, p, :, :].rearrange("p t n -> p (t n)"),
                         rc_table[bass.ds(b, 1)].rearrange("o t n -> o (t n)").to_broadcast([P, R * P])
                         ).then_inc(rc_in[p], 16)

        def sp_store(sp, b, p, use, rows=P):
            sp.wait_ge(fin, b + 3)
            sp.dma_start(out[bass.ds(b * P, rows), :], os_[0:rows, p, :]).then_inc(stored[p], 16)
            sp.wait_ge(stored[p], (use + 1) * 16)
            sp.sem_inc(os_free, 1)

        def act_node(act, b, p):
            act.wait_ge(node_mm, b + 1)
            for k in range(K):
                last = nc.scalar.activation(dg[:, p, k, :], id16[:, :], ACT.Copy,
                                            scale=wmask[:, bass.ds(b, 1), k])
            last.then_inc(dg_ready, 1)

        def act_node_out(act, b, p):
            act.wait_ge(node_mm, b + 3)
            act.wait_ge(out_mm, b + 1)
            nc.scalar.activation(bs[0:40, p, :], bsel[0:40, bass.ds(b * P, P)], ACT.Copy)
            nc.scalar.activation(hN[:, p, :, :], node_ps[:, :, :], ACT.Copy,
                                 scale=1.0 / H_SCALE).then_inc(hn_ready, 1)

        def act_zero(act, b, r):
            act.wait_ge(scaled, b + 3)
            nc.scalar.activation(S[:, :, r * P:(r + 1) * P], zeros3, ACT.Copy).then_inc(zeroed, 1)

        def pe_node(pe, b, p):
            pe.wait_ge(dg_ready, b + 1)
            pe.wait_ge(hn_ready, b + 1)
            for half in range(2):
                kk = slice(half * K // 2, (half + 1) * K // 2)
                for part in range(2):
                    last = nc.tensor.matmul(node_ps[:, kk, :],
                                            hh[:, bass.ds(b, 1), part * D:(part + 1) * D].rearrange("p o d -> p (o d)"),
                                            dg[:, p, kk, :], start=(part == 0), stop=(part == 1))
            last.then_inc(node_mm, 1)

        def pe_out_node(pe, b, p):
            pe.wait_ge(hn_ready, b + 2)
            pe.wait_ge(fin, b + 2)
            for k in range(K):
                nc.tensor.matmul(out_ps[:, :], hN[:, p, k, :], w_all[:, R + k, :],
                                 start=(k == 0), stop=False)
            nc.tensor.matmul(out_ps[:, :], bs[0:40, p, :], bias[0:40, :], start=False, stop=False)

        def pe_out_edge(pe, b, p, half):
            if half == 0:
                pe.wait_ge(scaled, b + 3)
            for t in range(half * R // 2, (half + 1) * R // 2):
                last = nc.tensor.matmul(out_ps[:, :], Sn[:, p, t, :], w_all[:, t, :],
                                        start=False, stop=(t == R - 1))
            if half == 1:
                last.then_inc(out_mm, 1)

        def pe_out(pe, b, p):
            pe_out_node(pe, b, p)
            pe_out_edge(pe, b, p, 0)
            pe_out_edge(pe, b, p, 1)

        def dve_scale(dve, b, p, r, use):
            dve.wait_ge(rc_in[p], (use + 1) * 16)
            dve.wait_ge(out_mm, b + 1)
            dve.wait_ge(zeroed, b + 1)
            nc.vector.tensor_tensor(Sn[:, p, :, :], S[:, :, r * P:(r + 1) * P], rcb[:, p, :, :],
                                    ALU.mult).then_inc(scaled, 1)

        def dve_finish(dve, b, p):
            dve.wait_ge(out_mm, b + 3)
            dve.wait_ge(os_free, b + 1)
            nc.vector.scalar_tensor_tensor(os_[:, p, :], out_ps[:, :], 0.0,
                                           xs[:, bass.ds(b, 1), :].rearrange("p o d -> p (o d)"),
                                           ALU.max, ALU.add).then_inc(fin, 1)


        def windows(row, c0, n, engine):
            got = []
            for v in range(0, n, 4):
                m = min(4, n - v)
                got += nc.values_load_multi_w_load_instructions(
                    row[0:1, bass.ds(c0 + v, m)], engines=[engine], min_val=0,
                    max_val=(RING - 1 if row is ring_i else N - 1),
                    skip_runtime_bounds_check_because="dst is a node; the path's test bounds it")[1]
            return got

        def gather(pool, slot, index, done):
            nc.gpsimd.indirect_dma_start(
                out=G[:, slot, :], out_offset=None, in_=h_table[:, :],
                in_offset=bass.IndirectOffsetOnAxis(ap=index, axis=0)).then_inc(done, 16)

        block = ctx.enter_context(nc.Block())

        @block.sync
        def _(sp):
            sp.wait_ge(xpad_set, 1)
            for c in range(5):
                full = min(5, NB - 1 - 5 * c)
                sp.dma_start(xs[:, 5 * c:5 * c + full, :],
                             x[5 * c * P:(5 * c + full) * P, :].rearrange("(b p) d -> p b d", p=P)
                             ).then_inc(x_in[c], 16)
            sp.dma_start(xs[0:NLAST, NB - 1, :], x[(NB - 1) * P:N, :]).then_inc(x_in[4], 16)
            for c in range(5):
                sp.wait_ge(h_ready, c + 1)
                sp.dma_start(h_table[5 * c * P:5 * (c + 1) * P, :].rearrange("(b p) d -> p b d", p=P),
                             hh[:, 5 * c:5 * (c + 1), :]).then_inc(h_stored, 16)
            sp.dma_start(w_all[:, 0:R, :], w_edge.rearrange("t d f -> d t f")).then_inc(w_in, 16)
            sp.dma_start(w_all[:, R:R + K, :], w_node.rearrange("t d f -> d t f")).then_inc(w_in, 16)
            sp.wait_ge(consts, 2)
            sp.dma_start(bias[0:R, :], b_edge[:, :]).then_inc(w_in, 16)
            sp.dma_start(bias[32:32 + K, :], b_node[:, :]).then_inc(w_in, 16)
            sp.wait_ge(flag_ready, 1)
            bad = sp.value_load(flag[0:1, 0:1], min_val=0, max_val=FLAG_MAX)
            with sp.If(bad < 1):
                sp.wait_ge(cnt_ready, 1)
                sp.dma_start(cnt_table.rearrange("b t n -> t b n"),
                             cnt[:, 0:NB * P].rearrange("t (b n) -> t b n", n=P)).then_inc(cnt_moved, 16)
                sp.wait_ge(cnt_moved, 16)
                wide = "b t n -> (b t n)"
                sp.dma_start(rc_w, cnt_table.rearrange(wide).rearrange("(p c) -> p c", p=P)).then_inc(cnt_moved, 16)
                sp.wait_ge(rc_ready, 1)
                sp.dma_start(rc_table.rearrange(wide).rearrange("(p c) -> p c", p=P), rc_w).then_inc(rc_stored, 16)
                sp.wait_ge(rc_stored, 16)

                def body(i, first):
                    for g in range(4):
                        sp_load_rc(sp, 4 * i + g, g % 2)
                        if not (first and g == 0):
                            sp_store(sp, 4 * i + g - 1, (g - 1) % 2, 2 * i + (g - 1) // 2)
                body(0, True)
                with sp.Fori(1, ITERS) as i:
                    body(i, False)
                sp_load_rc(sp, NB - 1, 0)
                sp_store(sp, NB - 2, 1, (NB - 2) // 2)
                sp_store(sp, NB - 1, 0, (NB - 1) // 2, NLAST)
            with sp.Else():
                def one(b, p, use, rows=P):
                    sp.wait_ge(g_rc, b + 1)
                    sp.dma_start(rc_table[bass.ds(b, 1)].rearrange("o t n -> (o t) n"),
                                 grc[:, :]).then_inc(g_rcst, 16)
                    sp.wait_ge(g_rcst, (b + 1) * 16)
                    sp_load_rc(sp, b, p)
                    sp_store(sp, b, p, use, rows)
                with sp.Fori(0, (NB - 1) // 2) as i:
                    one(2 * i, 0, i)
                    one(2 * i + 1, 1, i)
                one(NB - 1, 0, (NB - 1) // 2, NLAST)
            sp.wait_ge(stored[0], 16 * ((NB + 1) // 2))
            sp.wait_ge(stored[1], 16 * (NB // 2))

        @block.gpsimd
        def _(pool):
            nc.gpsimd.memset(ones[:, :], 1.0)
            nc.gpsimd.memset(zcol[:, :], 0.0)
            nc.gpsimd.memset(id32[:, :], 0.0).then_inc(consts, 1)
            nc.gpsimd.memset(bias[:, :], 0.0).then_inc(consts, 1)
            pool.wait_ge(consts, 1)
            nc.gpsimd.affine_select(out=id32[:, :], in_=id32[:, :], compare_op=ALU.not_equal, fill=1.0,
                                    base=0, pattern=[[-1, P]], channel_multiplier=1).then_inc(consts, 1)
            pool.wait_ge(consts, 3)
            nc.gpsimd.tensor_copy(id16[:, :], id32[:, :]).then_inc(consts, 1)
            with nc.allow_low_precision(reason="integers up to 2048 are exact in float16"):
                nc.gpsimd.iota(iota[:, :], pattern=[[1, R * P + 1]], base=0, channel_multiplier=0,
                               allow_small_or_imprecise_dtypes=True)
            nc.gpsimd.iota(pair16[:, :], pattern=[[16, PAIRS]], base=0, channel_multiplier=0,
                           allow_small_or_imprecise_dtypes=True).then_inc(consts, 1)
            pool.wait_ge(consts, 5)
            nc.gpsimd.iota(kcol[32:64, :], pattern=[[0, 1]], base=0, channel_multiplier=1,
                           allow_small_or_imprecise_dtypes=True).then_inc(consts, 1)
            pool.wait_ge(consts, 6)
            nc.gpsimd.memset(S[:, :, :], 0.0).then_inc(zeroed_s, 1)
            nc.gpsimd.memset(bsel[0:64, :], 0.0).then_inc(zeroed_s, 1)

            pool.wait_ge(src_ready, 1)
            pool.wait_ge(h_stored, 16 * 5)
            for j in range(LATE):
                for a in range(2):
                    gather(pool, 2 * (BODY + j) + a, src_t[:, 2 * j + a:2 * j + a + 1], gathered_p[j])
            pool.wait_ge(flag_ready, 1)
            bad = pool.value_load(flag[0:1, 0:1], min_val=0, max_val=FLAG_MAX)
            pool.wait_ge(mask_ready, 1)
            with pool.If(bad < 1):
                def may_issue():
                    pool.sem_inc(issuing, 1)
                with pool.Fori(0, ITERS) as i:
                    for u in range(BODY):
                        if u % PPB == 0:
                            pool.wait_ge(pair_mm, LATE + BODY * i + u + PPB)
                        if u % (BODY // 2) == 0:
                            pool.wait_ge(staged, 2 * i + u // (BODY // 2) + 1)
                        if u % PPB == 0:
                            may_issue()
                        for a in range(2):
                            gather(pool, 2 * u + a, src_s[:, 2 * u + a:2 * u + a + 1], gathered[u])
                pool.wait_ge(pair_mm, LATE + BODY * ITERS + PPB)
                j = PAIRS - 1
                for a in range(2):
                    gather(pool, a, src_t[:, 2 * j + a:2 * j + a + 1], gathered[0])
            with pool.Else():
                for s in range(0, NB, SEG):
                    with pool.Fori(0, min(SEG, NB - s) * NT) as n:
                        pool.wait_ge(g_src, s * NT + n + 1)
                        pool.sem_inc(issuing, 1)
                        gather(pool, 0, src_s[:, 0:1], g_rows[s // SEG])
                        pool.wait_ge(g_rows[s // SEG], (n + 1) * 16)

        PARTS = [slice(0, 15), slice(15, NB)]

        @block.scalar
        def _(act):
            act.wait_ge(xpad_set, 1)
            row = 0
            for arr in (src, dst, etype):
                act.dma_start(meta_i[:, row:row + CH - 1, :],
                              arr[0:(CH - 1) * P * P].rearrange("(c p e) -> p c e", p=P, e=P)
                              ).then_inc(meta_in, 16)
                full = NTF - (CH - 1) * P
                act.dma_start(meta_i[0:full, row + CH - 1, :],
                              arr[(CH - 1) * P * P:NTF * P].rearrange("(p e) -> p e", e=P)
                              ).then_inc(meta_in, 16)
                act.dma_start(meta_i[full:full + 1, row + CH - 1, 0:ELAST],
                              arr[NTF * P:E].rearrange("(o e) -> o e", o=1)).then_inc(meta_in, 16)
                row += CH
            act.dma_start(meta_i[0:NB - 1, row, :],
                          ntype[0:(NB - 1) * P].rearrange("(p e) -> p e", e=P)).then_inc(meta_in, 16)
            act.dma_start(meta_i[NB - 1:NB, row, 0:NLAST],
                          ntype[(NB - 1) * P:N].rearrange("(o e) -> o e", o=1)).then_inc(meta_in, 16)
            act.dma_start(nt_row[32:32 + K, 0:N],
                          ntype.rearrange("(o n) -> o n", o=1).to_broadcast([K, N])).then_inc(ntrow_in, 16)
            act.wait_ge(meta_in, 16 * 11)
            nc.scalar.activation(meta_f[:, :, :], meta_i[:, :, :], ACT.Copy).then_inc(meta_cast, 1)

            def std(part):
                act.wait_ge(var_ready, part + 1)
                nc.scalar.activation(rstd[:, 1, PARTS[part]], rstd[:, 0, PARTS[part]],
                                     ACT.Sqrt).then_inc(std_ready, 1)
            std(0)
            act.wait_ge(meta_tr, 1)
            nc.scalar.activation(src_t[:, :], acc[0][:, 0:TC], ACT.Copy).then_inc(src_ready, 1)
            for c in range(5):
                if c == 2:
                    std(1)
                act.wait_ge(rstd_ready, 1 if c < 3 else 2)
                for b in range(5 * c, 5 * c + 5):
                    last = nc.scalar.activation(ynorm[:, b, :], ynorm[:, b, :], ACT.Relu, scale=rstd[:, 3, b:b + 1])
                last.then_inc(relu_done, 1)
            for s in (zeroed, hn_ready):
                act.sem_inc(s, 1)
            act.wait_ge(consts, 6)
            act.wait_ge(meta_tr, 4)
            act.wait_ge(h_ready, 5)
            for buf in cnt_q:
                nc.scalar.activation(buf, zcol[0:R, :].to_broadcast([R, CN]), ACT.Copy).then_inc(cnt_zeroed, 1)
            act.wait_ge(src_ready, 1)
            act.wait_ge(flag_ready, 1)
            bad = act.value_load(flag[0:1, 0:1], min_val=0, max_val=FLAG_MAX)
            with act.If(bad < 1):
                H = BODY // 2

                def stage(i, half):
                    c0 = 2 * LATE + 2 * BODY * i + 2 * H * half
                    nc.scalar.activation(src_s[:, 2 * H * half:2 * H * (half + 1)],
                                         src_t[:, bass.ds(c0, 2 * H)], ACT.Copy)
                    nc.scalar.activation(seg_s[:, 2 * H * half:2 * H * (half + 1)],
                                         seg[:, bass.ds(c0, 2 * H)], ACT.Copy).then_inc(staged, 1)
                stage(0, 0)
                stage(0, 1)
                act.wait_ge(cnt_zeroed, 2)
                with act.Fori(0, CITERS) as i:
                    for q in range(2):
                        batch = 2 * i + q
                        at = windows(quad_i, batch * CB, CB, mybir.EngineType.Activation)
                        act.wait_ge(c_mm, batch + 2)
                        for v in range(CB):
                            last = nc.scalar.activation(cnt_q[(q + v) % 2][:, bass.ds(at[v], WQ)],
                                                        acc[2 + q][0:R, v * WQ:(v + 1) * WQ], ACT.Copy)
                        last.then_inc(c_out, 1)
                act.wait_ge(mask_ready, 1)
                act_node(act, 0, 0)
                act.wait_ge(ind_ready, 1)
                with act.Fori(0, ITERS) as i:
                    for g in range(4):
                        b = 4 * i + g
                        act_node_out(act, b, g % 2)
                        act_node(act, b + 1, (g + 1) % 2)
                        if g % 2 == 1:
                            act.wait_ge(pair_mm, BODY + LATE + BODY * i + (g + 1) * PPB)
                            stage(i + 1, g // 2)
                        act_zero(act, b, g)
                act_node_out(act, NB - 1, 0)
            with act.Else():
                act.wait_ge(mask_ready, 1)

                def sweep(b):
                    with act.Fori(0, NT) as t:
                        n = b * NT + t
                        act.wait_ge(g_mm, n + 1)
                        nc.scalar.activation(src_s[:, 0:1], src_t[:, bass.ds(t, 1)],
                                             ACT.Copy).then_inc(g_src, 1)

                def one(b, p):
                    sweep(b)
                    act_node(act, b, p)
                    act.wait_ge(g_rc, b + 1)
                    act_node_out(act, b, p)
                    act_zero(act, b, p)
                with act.Fori(0, (NB - 1) // 2) as i:
                    one(2 * i, 0)
                    one(2 * i + 1, 1)
                one(NB - 1, 0)

        @block.tensor
        def _(pe):
            pe.wait_ge(consts, 3)
            pe.wait_ge(meta_cast, 1)
            for a in range(3):
                for c in range(CH):
                    last = nc.tensor.transpose(acc[a][:, c * P:(c + 1) * P], meta_f[:, a * CH + c, :], id32[:, :])
                last.then_inc(meta_tr, 1)
            nc.tensor.transpose(misc[:, 0:P], meta_f[:, 3 * CH, :], id32[:, :]).then_inc(meta_tr, 1)
            pe.wait_ge(dst_out, 1)
            nc.tensor.matmul(acc[3][:, 0:TC // 2], ones[0:1, :], dst_t[0:1, 0:TC:2],
                             start=True, stop=True).then_inc(base_bc, 1)
            pe.wait_ge(viol_ready, 1)
            nc.tensor.matmul(misc[0:1, 256:257], ones[:, 0:1], nviol[:, 0:1],
                             start=True, stop=True).then_inc(viol_sum, 1)
            pe.wait_ge(h_ready, 5)
            pe.wait_ge(src_ready, 1)
            for s in (node_mm, out_mm):
                pe.sem_inc(s, 2)
            pe.sem_inc(pair_mm, BODY)
            for s in (c_mm, g_mm):
                pe.sem_inc(s, 1)
            pe.wait_ge(flag_ready, 1)
            bad = pe.value_load(flag[0:1, 0:1], min_val=0, max_val=FLAG_MAX)
            with pe.If(bad < 1):
                with pe.Fori(0, CITERS) as i:
                    for q in range(2):
                        pe.wait_ge(c_oh, 2 * i + q + 1)
                        pe.wait_ge(c_out, 2 * i + q + 1)
                        for v in range(CB):
                            for a in range(4):
                                last = nc.tensor.matmul(acc[2 + q][0:R, v * WQ:(v + 1) * WQ],
                                                        tcnt[:, q, 4 * v + a, :], ncnt[:, q, 4 * v + a, :],
                                                        start=(a == 0), stop=(a == 3))
                        last.then_inc(c_mm, 1)
                pe.wait_ge(w_in, 64)

                def sums(pair, bank, g_slot, o, got, got_value, added):
                    pe.wait_ge(got, got_value)
                    pe.wait_ge(oh_ready, pair + 1)
                    if not (isinstance(added, int) and added == 0):
                        pe.wait_ge(s_add, added)
                    for a in range(2):
                        for part in range(2):
                            last = nc.tensor.matmul(acc[bank][:, 0:R * W],
                                                    G[:, 2 * g_slot + a, part * D:(part + 1) * D],
                                                    oh[:, o, a, :], start=(a + part == 0),
                                                    stop=(a + part == 2))
                    last.then_inc(pair_mm, 1)
                for j in range(LATE):
                    if j == 2:
                        pe.wait_ge(c_out, 2 * CITERS + 1)
                    sums(j, j, BODY + j, (j - LATE) % 4, gathered_p[j], 32, 0)
                pe_node(pe, 0, 0)

                def body(i, first):
                    for u in range(BODY):
                        added = u if first else LATE + i * PER + (u - 3 if u >= 4 else u - 5)
                        sums(i * BODY + LATE + u, (u + LATE) % 4, u, u % 4, gathered[u], 32 * i + 32, added)
                        g, v = u // PPB, u % PPB
                        before = not (first and g == 0)
                        if v == 1 and before:
                            pe_out_node(pe, 4 * i + g - 1, (g - 1) % 2)
                        if v == 3 and before:
                            pe_out_edge(pe, 4 * i + g - 1, (g - 1) % 2, 0)
                        if v == 5 and before:
                            pe_out_edge(pe, 4 * i + g - 1, (g - 1) % 2, 1)
                        if v == 6:
                            pe_node(pe, 4 * i + g + 1, (g + 1) % 2)
                body(0, True)
                with pe.Fori(1, ITERS) as i:
                    body(i, False)
                sums(PAIRS - 1, (PAIRS - 1) % 4, 0, 0, gathered[0], 32 * ITERS + 32,
                     LATE + (ITERS - 1) * PER + BODY - 3)
                pe_out(pe, NB - 2, 1)
                pe_out(pe, NB - 1, 0)
            with pe.Else():
                pe.wait_ge(w_in, 64)

                def tile(s, n, first, last_tile):
                    pe.wait_ge(g_rows[s // SEG], (n - s * NT + 1) * 16)
                    pe.wait_ge(g_oh, n + 1)
                    for q in range(4):
                        for part in range(2):
                            nc.tensor.matmul(acc[q][:, :], G[:, 0, part * D:(part + 1) * D],
                                             goh[:, q * 512:(q + 1) * 512],
                                             start=first and part == 0, stop=last_tile and part == 1)
                    nc.tensor.matmul(misc[0:R, 0:P], gt[:, :], gn[:, :],
                                     start=first, stop=last_tile).then_inc(g_mm, 1)

                def one(s, b, p):
                    pe.wait_ge(g_blk, b + 1)
                    tile(s, b * NT, True, False)
                    with pe.Fori(1, NT - 1) as t:
                        tile(s, b * NT + t, False, False)
                    tile(s, b * NT + NT - 1, False, True)
                    pe_node(pe, b, p)
                    pe_out(pe, b, p)
                for s in range(0, NB - 1, SEG):
                    with pe.Fori(0, SEG // 2) as i:
                        one(s, s + 2 * i, 0)
                        one(s, s + 2 * i + 1, 1)
                one(NB - 1, NB - 1, 0)

        @block.vector
        def _(dve):
            steps = [0]

            def own(ins):
                ins.then_inc(vstep, 1)
                steps[0] += 1

            def settle():
                dve.wait_ge(vstep, steps[0])

            nc.vector.memset(xs[:, NB - 1, :], 0.0)
            for row, value in ((CH - 1, 0), (2 * CH - 1, N - 1), (3 * CH - 1, PADTYPE), (3 * CH, PADTYPE)):
                last = nc.vector.memset(meta_i[:, row, :], value)
            last.then_inc(xpad_set, 1)
            own(nc.vector.memset(nt_row[32:64, N:NB * P], PADTYPE))
            def chunk(c):
                bb = slice(5 * c, 5 * c + 5)
                dve.wait_ge(x_in[c], 32 if c == 4 else 16)
                for b in range(5 * c, 5 * c + 5):
                    own(nc.vector.bn_stats(stats[:, b, :], xs[:, b, :]))
                settle()
                for b in range(5 * c, 5 * c + 5):
                    own(nc.vector.bn_aggr(mv[:, b, :], stats[:, b, :]))
                settle()
                own(nc.vector.tensor_tensor(ynorm[:, bb, :], xs[:, bb, :],
                                            mv[:, bb, 0:1].to_broadcast([P, 5, D]), ALU.subtract))

            def variance(part):
                nc.vector.tensor_scalar(rstd[:, 0, PARTS[part]], mv[:, PARTS[part], 1], 1e-5, None,
                                        ALU.add).then_inc(var_ready, 1)

            def inverse(part):
                var, std, inv, r = (rstd[:, k, PARTS[part]] for k in range(4))
                dve.wait_ge(var_ready, part + 1)
                dve.wait_ge(std_ready, part + 1)
                own(nc.vector.reciprocal(inv, std))
                settle()
                own(nc.vector.tensor_tensor(r, inv, inv, ALU.mult))
                settle()
                own(nc.vector.tensor_tensor(r, r, var, ALU.mult))
                settle()
                own(nc.vector.tensor_scalar(r, r, -0.5 * H_SCALE, 1.5 * H_SCALE, ALU.mult, ALU.add))
                settle()
                nc.vector.tensor_tensor(r, r, inv, ALU.mult).then_inc(rstd_ready, 1)

            def split(c):
                bb = slice(5 * c, 5 * c + 5)
                dve.wait_ge(relu_done, c + 1)
                own(nc.vector.tensor_copy(hh[:, bb, 0:D], ynorm[:, bb, :]))
                settle()
                nc.vector.tensor_tensor(hh[:, bb, D:2 * D], ynorm[:, bb, :], hh[:, bb, 0:D],
                                        ALU.subtract).then_inc(h_ready, 1)
            for c in range(3):
                chunk(c)
            variance(0)
            chunk(3)
            inverse(0)
            chunk(4)
            variance(1)
            split(0)
            inverse(1)
            for c in range(1, 5):
                split(c)
            dve.wait_ge(meta_tr, 4)
            nc.vector.tensor_copy(dst_t[:, :], acc[1][:, :]).then_inc(dst_out, 1)
            own(nc.vector.tensor_copy(et_t[:, :], acc[2][:, :]))
            own(nc.vector.tensor_copy(et16[:, :], acc[2][:, 0:4 * QUADS]))
            own(nc.vector.tensor_copy(nt_t[:, :], misc[:, 0:NB]))
            dve.wait_ge(dst_out, 1)
            own(nc.vector.tensor_copy(base_i[:, :], dst_t[0:1, 0:TC:2]))
            own(nc.vector.tensor_copy(quad_i[:, :], dst_t[0:1, 0:4 * QUADS:4]))
            dve.wait_ge(base_bc, 1)
            own(nc.vector.tensor_copy(base_b[:, :], acc[3][:, 0:TC // 2]))
            settle()
            own(nc.vector.tensor_tensor(rel[:, :].rearrange("p (j a) -> p j a", a=2),
                                        dst_t[:, :].rearrange("p (j a) -> p j a", a=2),
                                        base_b[:, :].unsqueeze(2).to_broadcast([P, TC // 2, 2]), ALU.subtract))
            own(nc.vector.tensor_tensor(relq[:, :].rearrange("p (j a) -> p j a", a=4),
                                        dst_t[:, 0:4 * QUADS].rearrange("p (j a) -> p j a", a=4),
                                        base_b[:, 0:2 * QUADS:2].unsqueeze(2).to_broadcast([P, QUADS, 4]),
                                        ALU.subtract))
            own(nc.vector.tensor_scalar(ring_i[:, :], base_i[:, :], RING - 1, None, ALU.bitwise_and))
            V1 = 2 * PAIRS
            V2 = V1 + 4 * QUADS
            V3 = V2 + PAIRS
            V4 = V3 + QUADS - 2
            dve.wait_ge(consts, 6)
            own(nc.vector.tensor_tensor(viol[:, V4:V4 + PAIRS], base_b[:, 0:PAIRS], pair16[:, :], ALU.subtract))
            own(nc.vector.tensor_tensor(viol[:, V3:V4], base_b[:, 4:2 * QUADS:2], base_b[:, 0:2 * QUADS - 4:2],
                                        ALU.subtract))
            settle()
            own(nc.vector.scalar_tensor_tensor(seg[:, :], et_t[:, :], float(W), rel[:, :], ALU.mult, ALU.add))
            own(nc.vector.tensor_scalar(viol[:, 0:V1], rel[:, 0:V1], 0.0, None, ALU.is_lt))
            own(nc.vector.tensor_scalar(viol[:, V1:V2], relq[:, :], 0.0, None, ALU.is_lt))
            own(nc.vector.tensor_scalar(viol[:, V2:V3], viol[:, V4:V4 + PAIRS], -16.0 * LATE, None, ALU.is_lt))
            own(nc.vector.tensor_scalar(viol[:, V3:V4], viol[:, V3:V4], float(WQ), None, ALU.is_lt))
            settle()
            own(nc.vector.scalar_tensor_tensor(viol[:, 0:V1], rel[:, 0:V1], float(W - 1), viol[:, 0:V1],
                                               ALU.is_gt, ALU.add))
            own(nc.vector.scalar_tensor_tensor(viol[:, V1:V2], relq[:, :], float(WQ - 1), viol[:, V1:V2],
                                               ALU.is_gt, ALU.add))
            own(nc.vector.scalar_tensor_tensor(viol[:, V2:V3], viol[:, V4:V4 + PAIRS], float(AHEAD),
                                               viol[:, V2:V3], ALU.is_gt, ALU.add))
            settle()
            nc.vector.tensor_reduce(nviol[:, 0:1], viol[:, 0:V4], AX.X, ALU.add).then_inc(viol_ready, 1)
            dve.wait_ge(viol_sum, 1)
            nc.vector.tensor_copy(flag[:, :], misc[0:1, 256:257]).then_inc(flag_ready, 1)
            own(nc.vector.tensor_tensor(wmask[:, :, :], nt_t[:, :].unsqueeze(2).to_broadcast([P, NB, K]),
                                        iota_w[:, 0:K].unsqueeze(1).to_broadcast([P, NB, K]), ALU.is_equal))
            dve.wait_ge(ntrow_in, 16)
            dve.wait_ge(zeroed_s, 2)
            own(nc.vector.tensor_scalar(bsel[32:32 + K, :], nt_row[32:32 + K, :], kcol[32:32 + K, :], None,
                                        ALU.is_equal))
            settle()
            dve.sem_inc(mask_ready, 1)
            for s in (scaled, fin, os_free):
                dve.sem_inc(s, 2)
            for s in (c_out, g_blk):
                dve.sem_inc(s, 1)
            dve.wait_ge(flag_ready, 1)
            bad = dve.value_load(flag[0:1, 0:1], min_val=0, max_val=FLAG_MAX)

            def rc_of(rc, ind, count, steps_before, done):
                nc.vector.tensor_scalar(ind, count, 1.0, None, ALU.min).then_inc(cvec, 1)
                nc.vector.tensor_scalar(rc, count, 1.0, H_SCALE, ALU.max, ALU.mult).then_inc(cvec, 1)
                dve.wait_ge(cvec, steps_before + 2)
                nc.vector.reciprocal(rc, rc).then_inc(done, 1)

            with dve.If(bad < 1):
                DVE = mybir.EngineType.DVE
                def count_oh(batch, q):
                    c0 = batch * 4 * CB
                    nc.vector.tensor_tensor(tcnt[:, q, :, :],
                                            et16[:, bass.ds(c0, 4 * CB)].unsqueeze(2).to_broadcast([P, 4 * CB, R]),
                                            iota_w[:, 0:R].unsqueeze(1).to_broadcast([P, 4 * CB, R]), ALU.is_equal)
                    nc.vector.tensor_tensor(ncnt[:, q, :, :],
                                            relq[:, bass.ds(c0, 4 * CB)].unsqueeze(2).to_broadcast([P, 4 * CB, WQ]),
                                            iota_w[:, 0:WQ].unsqueeze(1).to_broadcast([P, 4 * CB, WQ]),
                                            ALU.is_equal).then_inc(c_oh, 1)

                count_oh(0, 0)
                count_oh(1, 1)
                with dve.Fori(1, CITERS) as i:
                    for q in range(2):
                        dve.wait_ge(c_mm, 2 * i + q)
                        count_oh(2 * i + q, q)

                def onehot(o, cols):
                    for a in range(2):
                        last = nc.vector.tensor_scalar(oh[:, o, a, :], iota_w[:, 0:R * W], cols[:, a:a + 1],
                                                       None, ALU.is_equal)
                    last.then_inc(oh_ready, 1)

                def add(pair, bank, at, adds):
                    dve.wait_ge(pair_mm, BODY + pair + 1)
                    dve.wait_ge(s_add, adds)
                    span = S[:, :, bass.ds(at, W)]
                    nc.vector.tensor_tensor(span, span,
                                            acc[bank][:, 0:R * W].rearrange("p (t n) -> p t n", n=W),
                                            ALU.add).then_inc(s_add, 1)
                onehot(1, seg[:, 0:2])
                onehot(2, seg[:, 2:4])
                onehot(3, seg[:, 4:6])
                dve.wait_ge(c_out, 2 * CITERS + 1)
                dve.wait_ge(cnt_zeroed, 2)
                nc.vector.tensor_tensor(cnt[:, 0:NB * P], cnt[:, 0:NB * P], cnt_q[1][:, 0:NB * P],
                                        ALU.add).then_inc(cnt_ready, 1)
                dve.wait_ge(cnt_ready, 1)
                nc.vector.tensor_scalar(bsel[0:R, :], cnt[:, 0:NB * P], 1.0, None, ALU.min).then_inc(ind_ready, 1)
                at = windows(ring_i, 0, LATE, DVE)
                dve.wait_ge(staged, 1)
                for j in range(LATE):
                    onehot(j, seg_s[:, 2 * j:2 * j + 2])
                    add(j, j, at[j], j)
                dve.wait_ge(cnt_moved, 32)
                nc.vector.tensor_scalar(rc_w, rc_w, 1.0, H_SCALE, ALU.max, ALU.mult).then_inc(cvec, 1)
                dve.wait_ge(cvec, 1)
                nc.vector.reciprocal(rc_w, rc_w).then_inc(rc_ready, 1)

                def body(i, first):
                    n0 = LATE + i * PER
                    done = 0
                    for u in range(BODY):
                        pair = LATE + i * BODY + u
                        g, v = u // PPB, u % PPB
                        if u % 4 == 0:
                            at = windows(ring_i, LATE + i * BODY + u, 4, DVE)
                        if u == BODY // 2 - 3:
                            dve.wait_ge(staged, 2 * i + 2)
                        if u == BODY - 3:
                            dve.wait_ge(staged, 2 * i + 3)
                        w = (u + 3) % BODY
                        onehot(w % 4, seg_s[:, 2 * w:2 * w + 2])
                        add(pair, (u + LATE) % 4, at[u % 4], n0 + done)
                        done += 1
                        if u == BODY - 1:
                            dve.wait_ge(zeroed, 4 * i + g + 1)
                            dve.wait_ge(s_add, n0 + done)
                            nc.vector.tensor_tensor(S[:, :, 0:W], S[:, :, 0:W], S[:, :, RING:RING + W],
                                                    ALU.add).then_inc(s_add, 1)
                            done += 1
                            dve.wait_ge(s_add, n0 + done)
                            nc.vector.memset(S[:, :, RING:RING + W], 0.0).then_inc(s_add, 1)
                            done += 1
                        if v == PPB - 1:
                            dve.wait_ge(s_add, n0 + done)
                            dve_scale(dve, 4 * i + g, g % 2, g, 2 * i + g // 2)
                        if v == 6 and not (first and g == 0):
                            dve_finish(dve, 4 * i + g - 1, (g - 1) % 2)
                    assert done == PER
                body(0, True)
                with dve.Fori(1, ITERS) as i:
                    body(i, False)
                at = windows(ring_i, PAIRS - 1, 1, DVE)
                add(PAIRS - 1, (PAIRS - 1) % 4, at[0], LATE + ITERS * PER)
                dve.wait_ge(s_add, LATE + ITERS * PER + 1)
                dve_scale(dve, NB - 1, 0, 0, (NB - 1) // 2)
                dve_finish(dve, NB - 2, 1)
                dve_finish(dve, NB - 1, 0)
            with dve.Else():
                nc.vector.memset(bbase[:, 0:1], 0.0).then_inc(g_vec, 1)
                GV = 6

                def tile(b, t):
                    n = b * NT + t
                    v0 = 1 + b + n * GV

                    def done(k):
                        dve.wait_ge(g_vec, v0 + k)
                    dve.wait_ge(g_mm, n + 1)
                    done(0)
                    d, v, lo, hi, col = (gcol[:, k:k + 1] for k in range(5))
                    nc.vector.tensor_tensor(v, dst_t[:, bass.ds(t, 1)], bbase[:, 0:1],
                                            ALU.subtract).then_inc(g_vec, 1)
                    done(1)
                    nc.vector.tensor_scalar(lo, v, 0.0, None, ALU.is_ge).then_inc(g_vec, 1)
                    nc.vector.tensor_scalar(hi, v, float(P), None, ALU.is_lt).then_inc(g_vec, 1)
                    nc.vector.scalar_tensor_tensor(col, et_t[:, bass.ds(t, 1)], float(P), v,
                                                   ALU.mult, ALU.add).then_inc(g_vec, 1)
                    done(4)
                    nc.vector.scalar_tensor_tensor(d, col, 1.0, lo, ALU.add, ALU.mult).then_inc(g_vec, 1)
                    done(5)
                    nc.vector.tensor_tensor(d, d, hi, ALU.mult).then_inc(g_vec, 1)
                    done(6)
                    nc.vector.tensor_scalar(goh[:, :], iota1[:, :], d, None, ALU.is_equal)
                    nc.vector.tensor_scalar(gn[:, :], iota_w[:, 0:P], v, None, ALU.is_equal)
                    nc.vector.tensor_scalar(gt[:, :], iota_w[:, 0:R], et_t[:, bass.ds(t, 1)], None,
                                            ALU.is_equal).then_inc(g_oh, 1)

                def one(b, p, use):
                    with dve.Fori(0, NT) as t:
                        tile(b, t)
                    dve.wait_ge(g_mm, (b + 1) * NT + 1)
                    dve.wait_ge(zeroed, b + 1)
                    for q in range(4):
                        nc.vector.tensor_copy(S[:, 4 * q:4 * q + 4, p * P:(p + 1) * P],
                                              acc[q][:, :].rearrange("p (t n) -> p t n", n=P)
                                              ).then_inc(s_add, 1)
                    rc_of(grc[:, :], bsel[0:R, bass.ds(b * P, P)], misc[0:R, 0:P], 2 * b, g_rc)
                    dve.wait_ge(s_add, 4 * b + 4)
                    nc.vector.tensor_scalar(bbase[:, 0:1], bbase[:, 0:1], float(P), None,
                                            ALU.add).then_inc(g_vec, 1)
                    dve.sem_inc(g_blk, 1)
                    dve_scale(dve, b, p, p, use)
                    dve_finish(dve, b, p)
                with dve.Fori(0, (NB - 1) // 2) as i:
                    one(2 * i, 0, i)
                    one(2 * i + 1, 1, i)
                one(NB - 1, 0, (NB - 1) // 2)


_INS = ['x', 'src', 'dst', 'edge_type_16', 'node_type_8', 'L0_gnn_W_edge', 'L0_gnn_b_edge', 'L0_gnn_W_node',
        'L0_gnn_b_node']


def kernel(**inputs):
    import numpy as _np
    import concourse.bacc as _bacc
    from concourse import mybir as _mybir
    from concourse.bass_utils import run_bass_kernel_spmd as _run

    nc = _bacc.Bacc("TRN2", target_bir_lowering=False, num_devices=1)
    arrays, args = {}, []
    for name in _INS:
        a = _np.ascontiguousarray(inputs[name])
        arrays[f"in_{name}_dram"] = a
        args.append(nc.dram_tensor(f"in_{name}_dram", a.shape, _mybir.dt.from_np(a.dtype), kind="ExternalInput").ap())
    n, d = inputs['x'].shape
    args.append(nc.dram_tensor("out_0_dram", (n, d), _mybir.dt.float32, kind="ExternalOutput").ap())
    gnn_layer(nc, *args)
    r = _run(nc, [arrays], core_ids=[0])
    return r.results[0]["out_0_dram"]
```

```python
import concourse.bass as bass
from concourse import mybir
from contextlib import ExitStack

F32, F16, I32 = mybir.dt.float32, mybir.dt.float16, mybir.dt.int32
ALU = mybir.AluOpType
ACT = mybir.ActivationFunctionType
AX = mybir.AxisListType


def gnn_layer(nc, x, src, dst, etype, ntype, w_edge, b_edge, w_node, b_node, out):
    N, D = x.shape
    E = src.shape[0]
    R = w_edge.shape[0]
    K = w_node.shape[0]
    P = 128
    NB = (N + P - 1) // P
    SEG = 8
    NLAST = N - (NB - 1) * P
    NT = (E + P - 1) // P
    NTF = E // P
    ELAST = E - NTF * P
    CH = (NT + P - 1) // P
    TC = CH * P
    PAIRS = (NT + 1) // 2
    W = 24
    W0 = 14
    RING = 4 * P
    PPB = 8
    LATE = 3
    BODY = 4 * PPB
    ITERS = (PAIRS - LATE) // BODY
    assert PAIRS - LATE - ITERS * BODY == 1 and NB == 4 * ITERS + 1 and R * W <= 512
    AHEAD = 128
    H_SCALE = 4096.0
    MID = NB * P // 2
    assert MID <= 2048
    FETCH_PARTS = ((0, 9), (9, 17), (17, NB))
    assert 2 * (LATE + ITERS * BODY) <= NTF
    PADTYPE = 64
    PER = BODY + 2
    QUADS = (NT + 3) // 4
    WQ = 44
    CB = 7
    CA = 5
    CITERS = QUADS // (2 * CB)
    assert CITERS * 2 * CB == QUADS and 2 * QUADS == PAIRS and CB * WQ <= 512
    CN = NB * P + WQ
    RCW = NB * R * P // P

    h_table = nc.dram_tensor("h_table", (NB * P, 2 * D), F16, kind="Internal").ap()
    cnt_table = nc.dram_tensor("cnt_table", (NB, R, P), F32, kind="Internal").ap()
    rc_table = nc.dram_tensor("rc_table", (NB, R, P), F32, kind="Internal").ap()

    ctx = ExitStack()
    with ctx:
        def sb(name, shape, dt):
            return ctx.enter_context(nc.sbuf_tensor(name, shape, dt))

        def ps(name, shape, dt=F32):
            return ctx.enter_context(nc.psum_tensor(name, shape, dt))

        def sem(name):
            return ctx.enter_context(nc.semaphore(name))

        xs = sb("xs", [P, NB, D], F32)
        hh = sb("hh", [P, NB, 2 * D], F16)
        union_a = sb("union_a", [P, 2 * R * P], F32)
        hf = union_a[:, 0:NB * D].rearrange("p (b d) -> p b d", d=D)
        Sn = union_a[:, :].rearrange("p (q t n) -> p q t n", q=2, t=R)
        union_b = sb("union_b", [P, 2 * R * P], F32)
        MROWS = 3 * CH + 1
        meta_i = union_b[:, 0:MROWS * P].bitcast(I32).rearrange("p (c e) -> p c e", e=P)
        meta_f = union_b[:, MROWS * P:2 * MROWS * P].rearrange("p (c e) -> p c e", e=P)
        cnt_q = [union_b[0:R, 0:CN], union_a[0:R, 0:CN]]
        cnt = cnt_q[0]
        rc_w = union_a[:, CN:CN + RCW]
        rcb = union_b[:, :].rearrange("p (q t n) -> p q t n", q=2, t=R)
        stats = sb("stats", [P, NB, 6], F32)
        mv = sb("mv", [P, NB, 2], F32)
        rstd = sb("rstd", [P, NB], F32)
        nmr = sb("nmr", [P, NB], F32)
        vv = sb("vv", [P, 3, NB], F32)
        src_t = sb("src_t", [P, TC], I32)
        union_d = sb("union_d", [P, 3 * TC + QUADS], F32)
        dst_t = union_d[:, 0:TC]
        et_t = union_d[:, TC:2 * TC]
        nt_t = sb("nt_t", [P, NB], F32)
        quad_f = union_d[:, 3 * TC:]
        rel = union_d[:, 2 * TC:3 * TC]
        seg = sb("seg", [P, TC], F32)
        relq = sb("relq", [P, 4 * QUADS], F16)
        et16 = sb("et16", [P, 4 * QUADS], F16)
        nviol = sb("nviol", [P, 2], F32)
        base_i = sb("base_i", [1, TC // 2], I32)
        ring_i = sb("ring_i", [1, TC // 2], I32)
        quad_i = sb("quad_i", [1, QUADS], I32)
        flag = sb("flag", [1, 1], I32)
        pair16 = sb("pair16", [P, PAIRS], F32)
        iota = sb("iota", [P, R * P + 1], F16)
        iota_w = iota[:, 0:R * W]
        iota1 = iota[:, 1:R * P + 1]
        id32 = sb("id32", [P, P], F32)
        id16 = sb("id16", [P, P], F16)
        ones = sb("ones", [P, P], F32)
        kcol = sb("kcol", [P, 1], F32)
        wmask = sb("wmask", [P, NB, K], F32)
        w_all = sb("w_all", [P, R + K, D], F32)
        bias = sb("bias", [P, D], F32)
        bsel = sb("bsel", [P, NB * P], F32)
        S = sb("S", [P, R, RING + W], F32)
        G = sb("G", [P, 2 * (BODY + LATE), 2 * D], F16)
        src_s = sb("src_s", [P, 2 * BODY], I32)
        seg_s = sb("seg_s", [P, 2 * BODY], F32)
        oh = sb("oh", [P, 4, 2, R * W], F16)
        union_c = sb("union_c", [P, 8 * CB * (R + WQ)], F16)
        tcnt = union_c[:, 0:8 * CB * R].rearrange("p (q t c) -> p q t c", q=2, t=R)
        ncnt = union_c[:, 8 * CB * R:].rearrange("p (q n c) -> p q n c", q=2, n=WQ)
        count_of = oh[:, :, :, :].rearrange("p o a c -> p (o a c)")[:, 0:WQ * 4 * CB].rearrange(
            "p (n c) -> p n c", n=WQ)
        assert NB * P <= 8 * CB * (R + WQ)
        fetch = union_c[:, 0:NB * P].rearrange("p (b e) -> p b e", e=P)
        src_row = sb("src_row", [P, 2, P], I32)
        src_r16 = sb("src_r16", [P, 2, P], F16)
        node_col = sb("node_col", [P, NB], F32)
        node_of = union_d.bitcast(F16)[:, 0:NB * P].rearrange("p (b e) -> p b e", e=P)
        dg = sb("dg", [P, 2, K, P], F16)
        hN = sb("hN", [P, 2, K, P], F32)
        viol = hN[:, :, :, :].rearrange("p q k n -> p (q k n)")
        bs = sb("bs", [64, 2, P], F32)
        os_ = sb("os", [P, 2, D], F32)
        nt_row = G[:, :, :].rearrange("p s d -> p (s d)").bitcast(I32)[:, 0:NB * P]
        goh = G[:, 8:8 + R * P // (2 * D), :].rearrange("p s d -> p (s d)")
        grc = sb("grc", [R, P], F32)
        gn = sb("gn", [P, P], F16)
        gt = sb("gt", [P, R], F16)
        zcol = sb("zcol", [P, 1], F32)
        zeros3 = zcol[:, :].unsqueeze(2).to_broadcast([P, R, P])
        gcol = sb("gcol", [P, 6], F32)
        bbase = sb("bbase", [P, 2], F32)

        acc = [ps(f"acc{q}", [P, 512]) for q in range(4)]
        misc = ps("misc", [P, 512])
        node_ps = ps("node_ps", [P, K, P])
        out_ps = ps("out_ps", [P, P])

        xpad_set = sem("xpad_set")
        x_in = [sem(f"x_in{c}") for c in range(5)]
        meta_in = sem("meta_in")
        w_in = sem("w_in")
        ntrow_in = sem("ntrow_in")
        consts = sem("consts")
        vstep = sem("vstep")
        var_ready = sem("var_ready")
        std_ready = sem("std_ready")
        rstd_ready = sem("rstd_ready")
        hi_done = sem("hi_done")
        et_out = sem("et_out")
        relu_done = sem("relu_done")
        meta_cast = sem("meta_cast")
        cnt_zeroed = sem("cnt_zeroed")
        cnt_ready = sem("cnt_ready")
        cnt_moved = sem("cnt_moved")
        ind_ready = sem("ind_ready")
        meta_tr = sem("meta_tr")
        dst_out = sem("dst_out")
        base_bc = sem("base_bc")
        h_ready = sem("h_ready")
        h_stored = sem("h_stored")
        src_ready = sem("src_ready")
        seg_ready = sem("seg_ready")
        viol_ready = sem("viol_ready")
        viol_sum = sem("viol_sum")
        flag_ready = sem("flag_ready")
        zeroed_s = sem("zeroed_s")
        mask_ready = sem("mask_ready")
        cvec = sem("cvec")
        c_oh = sem("c_oh")
        c_mm = sem("c_mm")
        c_out = sem("c_out")
        c_out_v = sem("c_out_v")
        rc_ready = sem("rc_ready")
        rc_stored = sem("rc_stored")
        issuing = sem("issuing")
        gathered = [sem(f"gathered{u}") for u in range(BODY)]
        gathered_p = [sem(f"gathered_p{u}") for u in range(LATE)]
        staged = sem("staged")
        oh_ready = sem("oh_ready")
        pair_mm = sem("pair_mm")
        s_add = sem("s_add")
        rc_in = [sem("rc_in0"), sem("rc_in1")]
        scaled = sem("scaled")
        zeroed = sem("zeroed")
        dg_ready = sem("dg_ready")
        node_mm = sem("node_mm")
        hn_ready = sem("hn_ready")
        out_mm = sem("out_mm")
        fin = sem("fin")
        os_free = sem("os_free")
        row_in = [sem("row_in0"), sem("row_in1")]
        row_used = sem("row_used")
        count_set = sem("count_set")
        fetch_oh = sem("fetch_oh")
        fetch_mm = sem("fetch_mm")
        fetched = sem("fetched")
        stored = [sem("stored0"), sem("stored1")]
        g_src = sem("g_src")
        g_rows = [sem(f"g_rows{k}") for k in range(4)]
        g_vec = sem("g_vec")
        g_oh = sem("g_oh")
        g_mm = sem("g_mm")
        g_blk = sem("g_blk")
        g_rc = sem("g_rc")
        g_rcst = sem("g_rcst")

        FLAG_MAX = 1 << 20

        def sp_load_rc(sp, b, p):
            sp.wait_ge(scaled, b + 1)
            sp.dma_start(rcb[:, p, :, :].rearrange("p t n -> p (t n)"),
                         rc_table[bass.ds(b, 1)].rearrange("o t n -> o (t n)").to_broadcast([P, R * P])
                         ).then_inc(rc_in[p], 16)

        def sp_load_row(sp, b, p):
            sp.wait_ge(row_used, b + 1)
            tile = 2 * (LATE + PPB * b + PPB - 1) + 1
            sp.dma_start(src_row[:, p, :],
                         src[bass.ds(tile * P, P)].rearrange("(o e) -> o e", o=1).to_broadcast([P, P])
                         ).then_inc(row_in[p], 16)

        def dve_fetch(dve, b, p, use, part):
            if part == 0:
                dve.wait_ge(row_in[p], (use + 1) * 16)
                nc.vector.tensor_scalar(src_r16[:, p, :], src_row[:, p, :], float(-MID), None,
                                        ALU.add).then_inc(row_used, 1)
                dve.wait_ge(fetch_mm, b + 1)
                dve.wait_ge(row_used, b + 3)
            first, end = FETCH_PARTS[part]
            nc.vector.tensor_tensor(fetch[:, first:end, :],
                                    src_r16[:, p:p + 1, :].to_broadcast([P, end - first, P]),
                                    node_of[:, first:end, :], ALU.is_equal).then_inc(fetch_oh, 1)

        def pe_fetch(pe, b, part):
            pe.wait_ge(fetch_oh, 3 * b + part + 1)
            if part == 0:
                pe.wait_ge(fetched, b + 1)
            for k in range(*FETCH_PARTS[part]):
                last = nc.tensor.matmul(misc[:, 0:2 * D], fetch[:, k, :], hh[:, k, :],
                                        start=(k == 0), stop=(k == NB - 1))
            if part == 2:
                last.then_inc(fetch_mm, 1)

        def act_fetch(act, b, g):
            act.wait_ge(fetch_mm, b + 2)
            nc.scalar.activation(G[:, 2 * (PPB * g + PPB - 1) + 1, :], misc[:, 0:2 * D],
                                 ACT.Copy).then_inc(fetched, 1)

        def sp_store(sp, b, p, use, rows=P):
            sp.wait_ge(fin, b + 3)
            sp.dma_start(out[bass.ds(b * P, rows), :], os_[0:rows, p, :]).then_inc(stored[p], 16)
            sp.wait_ge(stored[p], (use + 1) * 16)
            sp.sem_inc(os_free, 1)

        def act_node(act, b, p):
            act.wait_ge(node_mm, b + 1)
            for k in range(K):
                last = nc.scalar.activation(dg[:, p, k, :], id16[:, :], ACT.Copy,
                                            scale=wmask[:, bass.ds(b, 1), k])
            last.then_inc(dg_ready, 1)

        def act_node_out(act, b, p):
            act.wait_ge(node_mm, b + 3)
            act.wait_ge(out_mm, b + 1)
            nc.scalar.activation(bs[0:40, p, :], bsel[0:40, bass.ds(b * P, P)], ACT.Copy)
            nc.scalar.activation(hN[:, p, :, :], node_ps[:, :, :], ACT.Copy,
                                 scale=1.0 / H_SCALE).then_inc(hn_ready, 1)

        def act_zero(act, b, r):
            act.wait_ge(scaled, b + 3)
            nc.scalar.activation(S[:, :, r * P:(r + 1) * P], zeros3, ACT.Copy).then_inc(zeroed, 1)

        def pe_node(pe, b, p):
            pe.wait_ge(dg_ready, b + 1)
            pe.wait_ge(hn_ready, b + 1)
            for half in range(2):
                kk = slice(half * K // 2, (half + 1) * K // 2)
                for part in range(2):
                    last = nc.tensor.matmul(node_ps[:, kk, :],
                                            hh[:, bass.ds(b, 1), part * D:(part + 1) * D].rearrange("p o d -> p (o d)"),
                                            dg[:, p, kk, :], start=(part == 0), stop=(part == 1))
            last.then_inc(node_mm, 1)

        def pe_out_node(pe, b, p, into=None, rows=P):
            into = out_ps if into is None else into
            pe.wait_ge(hn_ready, b + 2)
            if into is out_ps:
                pe.wait_ge(fin, b + 2)
            for k in range(K):
                nc.tensor.matmul(into[0:rows, 0:D], hN[:, p, k, 0:rows], w_all[:, R + k, :],
                                 start=(k == 0), stop=False)
            nc.tensor.matmul(into[0:rows, 0:D], bs[0:40, p, 0:rows], bias[0:40, :], start=False, stop=False)

        def pe_out_edge(pe, b, p, half, into=None, rows=P):
            into = out_ps if into is None else into
            if half == 0:
                pe.wait_ge(scaled, b + 3)
            for t in range(half * R // 2, (half + 1) * R // 2):
                last = nc.tensor.matmul(into[0:rows, 0:D], Sn[:, p, t, 0:rows], w_all[:, t, :],
                                        start=False, stop=(t == R - 1))
            if half == 1:
                last.then_inc(out_mm, 1)

        def pe_out(pe, b, p):
            pe_out_node(pe, b, p)
            pe_out_edge(pe, b, p, 0)
            pe_out_edge(pe, b, p, 1)

        def dve_scale(dve, b, p, r, use, rows=P):
            dve.wait_ge(rc_in[p], (use + 1) * 16)
            dve.wait_ge(out_mm, b + 1)
            if rows == P:
                dve.wait_ge(zeroed, b + 1)
            nc.vector.tensor_tensor(Sn[:, p, :, 0:rows], S[:, :, r * P:r * P + rows], rcb[:, p, :, 0:rows],
                                    ALU.mult).then_inc(scaled, 1)

        def dve_finish(dve, b, p, result=None, rows=P):
            result = out_ps if result is None else result
            dve.wait_ge(out_mm, b + 3)
            dve.wait_ge(os_free, b + 1)
            nc.vector.scalar_tensor_tensor(os_[0:rows, p, :], result[0:rows, 0:D], 0.0,
                                           xs[0:rows, bass.ds(b, 1), :].rearrange("p o d -> p (o d)"),
                                           ALU.max, ALU.add).then_inc(fin, 1)

        def windows(row, c0, n, engine):
            got = []
            for v in range(0, n, 4):
                m = min(4, n - v)
                got += nc.values_load_multi_w_load_instructions(
                    row[0:1, bass.ds(c0 + v, m)], engines=[engine], min_val=0,
                    max_val=(RING - 1 if row is ring_i else N - 1),
                    skip_runtime_bounds_check_because="dst is a node; the path's test bounds it")[1]
            return got

        def gather(pool, slot, index, done):
            nc.gpsimd.indirect_dma_start(
                out=G[:, slot, :], out_offset=None, in_=h_table[:, :],
                in_offset=bass.IndirectOffsetOnAxis(ap=index, axis=0)).then_inc(done, 16)

        block = ctx.enter_context(nc.Block())

        @block.sync
        def _(sp):
            sp.wait_ge(xpad_set, 1)
            for c in range(5):
                full = min(5, NB - 1 - 5 * c)
                sp.dma_start(xs[:, 5 * c:5 * c + full, :],
                             x[5 * c * P:(5 * c + full) * P, :].rearrange("(b p) d -> p b d", p=P)
                             ).then_inc(x_in[c], 16)
            sp.dma_start(xs[0:NLAST, NB - 1, :], x[(NB - 1) * P:N, :]).then_inc(x_in[4], 16)
            for k, c in enumerate((4, 0, 1, 2, 3)):
                sp.wait_ge(h_ready, k + 1)
                sp.dma_start(h_table[5 * c * P:5 * (c + 1) * P, :].rearrange("(b p) d -> p b d", p=P),
                             hh[:, 5 * c:5 * (c + 1), :]).then_inc(h_stored, 16)
            sp.dma_start(w_all[:, 0:R, :], w_edge.rearrange("t d f -> d t f")).then_inc(w_in, 16)
            sp.dma_start(w_all[:, R:R + K, :], w_node.rearrange("t d f -> d t f")).then_inc(w_in, 16)
            sp.wait_ge(consts, 2)
            sp.dma_start(bias[0:R, :], b_edge[:, :]).then_inc(w_in, 16)
            sp.dma_start(bias[32:32 + K, :], b_node[:, :]).then_inc(w_in, 16)
            sp.wait_ge(flag_ready, 1)
            bad = sp.value_load(flag[0:1, 0:1], min_val=0, max_val=FLAG_MAX)
            with sp.If(bad < 1):
                sp_load_row(sp, 0, 0)
                sp_load_row(sp, 1, 1)
                sp.wait_ge(cnt_ready, 1)
                sp.dma_start(cnt_table.rearrange("b t n -> t b n"),
                             cnt[:, 0:NB * P].rearrange("t (b n) -> t b n", n=P)).then_inc(cnt_moved, 16)
                sp.wait_ge(cnt_moved, 16)
                wide = "b t n -> (b t n)"
                sp.dma_start(rc_w, cnt_table.rearrange(wide).rearrange("(p c) -> p c", p=P)).then_inc(cnt_moved, 16)
                sp.wait_ge(rc_ready, 1)
                sp.dma_start(rc_table.rearrange(wide).rearrange("(p c) -> p c", p=P), rc_w).then_inc(rc_stored, 16)
                sp.wait_ge(rc_stored, 16)

                def body(i, first):
                    for g in range(4):
                        if not (first and g < 2):
                            sp_load_row(sp, 4 * i + g, g % 2)
                        sp_load_rc(sp, 4 * i + g, g % 2)
                        if not (first and g < 2):
                            sp_store(sp, 4 * i + g - 2, g % 2, 2 * i + g // 2 - 1)
                body(0, True)
                with sp.Fori(1, ITERS) as i:
                    body(i, False)
                sp_load_rc(sp, NB - 1, 0)
                for b in (NB - 3, NB - 2, NB - 1):
                    sp_store(sp, b, b % 2, b // 2, NLAST if b == NB - 1 else P)
            with sp.Else():
                def one(b, p, use, rows=P):
                    sp.wait_ge(g_rc, b + 1)
                    sp.dma_start(rc_table[bass.ds(b, 1)].rearrange("o t n -> (o t) n"),
                                 grc[:, :]).then_inc(g_rcst, 16)
                    sp.wait_ge(g_rcst, (b + 1) * 16)
                    sp_load_rc(sp, b, p)
                    sp_store(sp, b, p, use, rows)
                with sp.Fori(0, (NB - 1) // 2) as i:
                    one(2 * i, 0, i)
                    one(2 * i + 1, 1, i)
                one(NB - 1, 0, (NB - 1) // 2, NLAST)
            sp.wait_ge(stored[0], 16 * ((NB + 1) // 2))
            sp.wait_ge(stored[1], 16 * (NB // 2))

        @block.gpsimd
        def _(pool):
            nc.gpsimd.memset(ones[:, :], 1.0)
            nc.gpsimd.memset(zcol[:, :], 0.0)
            nc.gpsimd.memset(id32[:, :], 0.0).then_inc(consts, 1)
            nc.gpsimd.memset(bias[:, :], 0.0).then_inc(consts, 1)
            pool.wait_ge(consts, 1)
            nc.gpsimd.affine_select(out=id32[:, :], in_=id32[:, :], compare_op=ALU.not_equal, fill=1.0,
                                    base=0, pattern=[[-1, P]], channel_multiplier=1).then_inc(consts, 1)
            pool.wait_ge(consts, 3)
            nc.gpsimd.tensor_copy(id16[:, :], id32[:, :]).then_inc(consts, 1)
            with nc.allow_low_precision(reason="integers up to 2048 are exact in float16"):
                nc.gpsimd.iota(iota[:, :], pattern=[[1, R * P + 1]], base=0, channel_multiplier=0,
                               allow_small_or_imprecise_dtypes=True)
            nc.gpsimd.iota(pair16[:, :], pattern=[[16, PAIRS]], base=0, channel_multiplier=0,
                           allow_small_or_imprecise_dtypes=True).then_inc(consts, 1)
            pool.wait_ge(consts, 5)
            nc.gpsimd.iota(kcol[32:64, :], pattern=[[0, 1]], base=0, channel_multiplier=1,
                           allow_small_or_imprecise_dtypes=True).then_inc(consts, 1)
            pool.wait_ge(consts, 6)
            nc.gpsimd.iota(node_col[:, :], pattern=[[P, NB]], base=-MID, channel_multiplier=1,
                           allow_small_or_imprecise_dtypes=True)
            nc.gpsimd.memset(S[:, :, :], 0.0).then_inc(zeroed_s, 1)
            nc.gpsimd.memset(bsel[0:64, :], 0.0).then_inc(zeroed_s, 1)

            pool.wait_ge(src_ready, 1)
            pool.wait_ge(h_stored, 16 * 5)
            for j in range(LATE):
                for a in range(2):
                    gather(pool, 2 * (BODY + j) + a, src_t[:, 2 * j + a:2 * j + a + 1], gathered_p[j])
            pool.wait_ge(flag_ready, 1)
            bad = pool.value_load(flag[0:1, 0:1], min_val=0, max_val=FLAG_MAX)
            pool.wait_ge(mask_ready, 1)
            with pool.If(bad < 1):
                def may_issue():
                    pool.sem_inc(issuing, 1)
                with pool.Fori(0, ITERS) as i:
                    for u in range(BODY):
                        if u % PPB == 0:
                            pool.wait_ge(pair_mm, LATE + BODY * i + u + PPB)
                        if u % (BODY // 2) == 0:
                            pool.wait_ge(staged, 2 * i + u // (BODY // 2) + 1)
                        if u % PPB == 0:
                            may_issue()
                        for a in range(1 if u % PPB == PPB - 1 else 2):
                            gather(pool, 2 * u + a, src_s[:, 2 * u + a:2 * u + a + 1], gathered[u])
                pool.wait_ge(pair_mm, LATE + BODY * ITERS + PPB)
                j = PAIRS - 1
                for a in range(2):
                    gather(pool, a, src_t[:, 2 * j + a:2 * j + a + 1], gathered[0])
            with pool.Else():
                for s in range(0, NB, SEG):
                    with pool.Fori(0, min(SEG, NB - s) * NT) as n:
                        pool.wait_ge(g_src, s * NT + n + 1)
                        pool.sem_inc(issuing, 1)
                        gather(pool, 0, src_s[:, 0:1], g_rows[s // SEG])
                        pool.wait_ge(g_rows[s // SEG], (n + 1) * 16)

        PARTS = [slice(0, 15), slice(15, NB)]

        @block.scalar
        def _(act):
            act.wait_ge(xpad_set, 1)
            nc.scalar.activation(vv[:, 1, :], vv[:, 1, :], ACT.Sqrt)
            row = 0
            for arr in (src, dst, etype):
                act.dma_start(meta_i[:, row:row + CH - 1, :],
                              arr[0:(CH - 1) * P * P].rearrange("(c p e) -> p c e", p=P, e=P)
                              ).then_inc(meta_in, 16)
                full = NTF - (CH - 1) * P
                act.dma_start(meta_i[0:full, row + CH - 1, :],
                              arr[(CH - 1) * P * P:NTF * P].rearrange("(p e) -> p e", e=P)
                              ).then_inc(meta_in, 16)
                act.dma_start(meta_i[full:full + 1, row + CH - 1, 0:ELAST],
                              arr[NTF * P:E].rearrange("(o e) -> o e", o=1)).then_inc(meta_in, 16)
                row += CH
            act.dma_start(meta_i[0:NB - 1, row, :],
                          ntype[0:(NB - 1) * P].rearrange("(p e) -> p e", e=P)).then_inc(meta_in, 16)
            act.dma_start(meta_i[NB - 1:NB, row, 0:NLAST],
                          ntype[(NB - 1) * P:N].rearrange("(o e) -> o e", o=1)).then_inc(meta_in, 16)
            act.dma_start(nt_row[32:32 + K, 0:N],
                          ntype.rearrange("(o n) -> o n", o=1).to_broadcast([K, N])).then_inc(ntrow_in, 16)
            def relu(c):
                act.wait_ge(rstd_ready, 1 if c < 3 else 2)
                for b in range(5 * c, 5 * c + 5):
                    last = nc.scalar.activation(hf[:, b, :], xs[:, b, :], ACT.Relu, scale=rstd[:, b:b + 1],
                                                bias=nmr[:, b:b + 1])
                last.then_inc(relu_done, 1)

            def high(c):
                act.wait_ge(relu_done, c + 1)
                nc.scalar.activation(hh[:, 5 * c:5 * c + 5, 0:D], hf[:, 5 * c:5 * c + 5, :],
                                     ACT.Copy).then_inc(hi_done, 1)
            def std(part):
                act.wait_ge(var_ready, part + 1)
                nc.scalar.activation(vv[:, 2, PARTS[part]], vv[:, 0, PARTS[part]], ACT.Sqrt).then_inc(std_ready, 1)

            std(0)
            relu(0)
            std(1)
            relu(1)
            relu(2)
            act.wait_ge(meta_tr, 2)
            nc.scalar.activation(dst_t[:, :], acc[1][:, :], ACT.Copy).then_inc(dst_out, 1)
            relu(3)
            high(2)
            high(3)
            nc.scalar.activation(src_t[:, :], acc[0][:, 0:TC], ACT.Copy).then_inc(src_ready, 1)
            act.wait_ge(meta_tr, 4)
            nc.scalar.activation(et_t[:, :], acc[2][:, :], ACT.Copy).then_inc(et_out, 1)
            nc.scalar.activation(et16[:, :], acc[2][:, 0:4 * QUADS], ACT.Copy).then_inc(et_out, 1)
            nc.scalar.activation(nt_t[:, :], misc[:, 0:NB], ACT.Copy).then_inc(et_out, 1)
            for s in (zeroed, hn_ready, fetched):
                act.sem_inc(s, 1)
            act.wait_ge(consts, 6)
            act.wait_ge(meta_tr, 4)
            act.wait_ge(h_ready, 5)
            nc.scalar.activation(count_of, iota_w[:, 0:WQ].unsqueeze(2).to_broadcast([P, WQ, 4 * CB]),
                                 ACT.Copy).then_inc(count_set, 1)
            for buf in cnt_q:
                nc.scalar.activation(buf, zcol[0:R, :].to_broadcast([R, CN]), ACT.Copy).then_inc(cnt_zeroed, 1)
            act.wait_ge(src_ready, 1)
            act.wait_ge(flag_ready, 1)
            bad = act.value_load(flag[0:1, 0:1], min_val=0, max_val=FLAG_MAX)
            with act.If(bad < 1):
                H = BODY // 2

                def stage(i, half):
                    c0 = 2 * LATE + 2 * BODY * i + 2 * H * half
                    nc.scalar.activation(src_s[:, 2 * H * half:2 * H * (half + 1)],
                                         src_t[:, bass.ds(c0, 2 * H)], ACT.Copy)
                    nc.scalar.activation(seg_s[:, 2 * H * half:2 * H * (half + 1)],
                                         seg[:, bass.ds(c0, 2 * H)], ACT.Copy).then_inc(staged, 1)
                act.wait_ge(seg_ready, 1)
                stage(0, 0)
                stage(0, 1)
                act.wait_ge(cnt_zeroed, 2)
                with act.Fori(0, CITERS) as i:
                    for q in range(2):
                        batch = 2 * i + q
                        at = windows(quad_i, batch * CB, CA, mybir.EngineType.Activation)
                        act.wait_ge(c_mm, batch + 2)
                        for v in range(CA):
                            last = nc.scalar.activation(cnt_q[(q + v) % 2][:, bass.ds(at[v], WQ)],
                                                        acc[2 + q][0:R, v * WQ:(v + 1) * WQ], ACT.Copy)
                        last.then_inc(c_out, 1)
                act.wait_ge(mask_ready, 1)
                act_node(act, 0, 0)
                nc.scalar.activation(node_of, node_col[:, :].unsqueeze(2).to_broadcast([P, NB, P]),
                                     ACT.Copy).then_inc(count_set, 1)
                act.wait_ge(ind_ready, 1)

                def body(i, first):
                    for g in range(4):
                        b = 4 * i + g
                        act_node_out(act, b, g % 2)
                        if not (first and g == 0):
                            act_zero(act, b - 1, (g - 1) % 4)
                        act_node(act, b + 1, (g + 1) % 2)
                        act_fetch(act, b, g)
                        if g % 2 == 1:
                            act.wait_ge(pair_mm, BODY + LATE + BODY * i + (g + 1) * PPB)
                            stage(i + 1, g // 2)
                body(0, True)
                with act.Fori(1, ITERS) as i:
                    body(i, False)
                act_node_out(act, NB - 1, 0)
            with act.Else():
                act.wait_ge(mask_ready, 1)

                def sweep(b):
                    with act.Fori(0, NT) as t:
                        n = b * NT + t
                        act.wait_ge(g_mm, n + 1)
                        nc.scalar.activation(src_s[:, 0:1], src_t[:, bass.ds(t, 1)],
                                             ACT.Copy).then_inc(g_src, 1)

                def one(b, p):
                    sweep(b)
                    act_node(act, b, p)
                    act.wait_ge(g_rc, b + 1)
                    act_node_out(act, b, p)
                    act_zero(act, b, p)
                with act.Fori(0, (NB - 1) // 2) as i:
                    one(2 * i, 0)
                    one(2 * i + 1, 1)
                one(NB - 1, 0)

        @block.tensor
        def _(pe):
            pe.wait_ge(consts, 3)
            pe.wait_ge(meta_cast, 1)
            for a in range(3):
                for c in range(CH):
                    last = nc.tensor.transpose(acc[a][:, c * P:(c + 1) * P], meta_f[:, a * CH + c, :], id32[:, :])
                last.then_inc(meta_tr, 1)
            nc.tensor.transpose(misc[:, 0:P], meta_f[:, 3 * CH, :], id32[:, :]).then_inc(meta_tr, 1)
            pe.wait_ge(dst_out, 1)
            nc.tensor.matmul(acc[3][:, 0:TC // 2], ones[0:1, :], dst_t[0:1, 0:TC:2],
                             start=True, stop=True).then_inc(base_bc, 1)
            pe.wait_ge(viol_ready, 1)
            pe.wait_ge(et_out, 3)
            nc.tensor.matmul(misc[0:1, 256:257], ones[:, 0:1], nviol[:, 1:2],
                             start=True, stop=True).then_inc(viol_sum, 1)
            pe.wait_ge(h_ready, 5)
            pe.wait_ge(src_ready, 1)
            for s in (node_mm, out_mm):
                pe.sem_inc(s, 2)
            pe.sem_inc(fetch_mm, 1)
            pe.sem_inc(pair_mm, BODY)
            for s in (c_mm, g_mm):
                pe.sem_inc(s, 1)
            pe.wait_ge(flag_ready, 1)
            bad = pe.value_load(flag[0:1, 0:1], min_val=0, max_val=FLAG_MAX)
            with pe.If(bad < 1):
                def count(i, first):
                    for q in range(2):
                        pe.wait_ge(c_oh, 2 * i + q + 1)
                        if not first:
                            pe.wait_ge(c_out, 2 * i + q)
                            pe.wait_ge(c_out_v, 2 * i + q)
                        for v in range(CB):
                            for a in range(4):
                                bank = acc[2 + q] if v < CA else acc[q]
                                last = nc.tensor.matmul(bank[0:R, v * WQ:(v + 1) * WQ],
                                                        tcnt[:, q, :, 4 * v + a], ncnt[:, q, :, 4 * v + a],
                                                        start=(a == 0), stop=(a == 3))
                        last.then_inc(c_mm, 1)
                count(0, True)
                with pe.Fori(1, CITERS) as i:
                    count(i, False)
                pe.wait_ge(w_in, 64)

                def sums(pair, bank, g_slot, o, got, got_value, added):
                    pe.wait_ge(got, got_value)
                    pe.wait_ge(oh_ready, pair + 1)
                    if not (isinstance(added, int) and added == 0):
                        pe.wait_ge(s_add, added)
                    window = acc[bank][:, 0:R * W].rearrange("p (t n) -> p t n", n=W)
                    for a, w in ((1, W), (0, W0)):
                        for part in range(2):
                            last = nc.tensor.matmul(window[:, :, 0:w],
                                                    G[:, 2 * g_slot + a, part * D:(part + 1) * D],
                                                    oh[:, o, a, 0:R * w].rearrange("p (t n) -> p t n", n=w),
                                                    start=(a == 1 and part == 0), stop=(a == 0 and part == 1))
                    last.then_inc(pair_mm, 1)
                pe.wait_ge(c_out_v, 2 * CITERS + 1)
                for j in range(LATE):
                    if j == 2:
                        pe.wait_ge(c_out, 2 * CITERS + 1)
                    sums(j, j, BODY + j, (j - LATE) % 4, gathered_p[j], 32, 0)
                pe_node(pe, 0, 0)

                def body(i, first):
                    for u in range(BODY):
                        if u % PPB == PPB - 1:
                            pe.wait_ge(fetched, 4 * i + u // PPB + 2)
                        added = u if first else LATE + i * PER + (u - 3 if u >= 4 else u - 5)
                        sums(i * BODY + LATE + u, (u + LATE) % 4, u, u % 4, gathered[u],
                             16 * i + 16 if u % PPB == PPB - 1 else 32 * i + 32, added)
                        g, v = u // PPB, u % PPB
                        before = not (first and g == 0)
                        if v == 0 and before:
                            pe_out_node(pe, 4 * i + g - 1, (g - 1) % 2)
                        if v == 2 and before:
                            pe_out_edge(pe, 4 * i + g - 1, (g - 1) % 2, 0)
                        if v == 3 and before:
                            pe_out_edge(pe, 4 * i + g - 1, (g - 1) % 2, 1)
                        if v in (4, 5, 6):
                            pe_fetch(pe, 4 * i + g, v - 4)
                        if v == 6:
                            pe_node(pe, 4 * i + g + 1, (g + 1) % 2)
                body(0, True)
                with pe.Fori(1, ITERS) as i:
                    body(i, False)
                pe_out_node(pe, NB - 2, 1)
                pe_out_node(pe, NB - 1, 0, misc, NLAST)
                sums(PAIRS - 1, (PAIRS - 1) % 4, 0, 0, gathered[0], 32 * ITERS + 32,
                     LATE + (ITERS - 1) * PER + BODY - 3)
                for b, p, into, rows in ((NB - 2, 1, out_ps, P), (NB - 1, 0, misc, NLAST)):
                    for half in range(2):
                        pe_out_edge(pe, b, p, half, into, rows)
            with pe.Else():
                pe.wait_ge(w_in, 64)

                def tile(s, n, first, last_tile):
                    pe.wait_ge(g_rows[s // SEG], (n - s * NT + 1) * 16)
                    pe.wait_ge(g_oh, n + 1)
                    for q in range(4):
                        for part in range(2):
                            nc.tensor.matmul(acc[q][:, :], G[:, 0, part * D:(part + 1) * D],
                                             goh[:, q * 512:(q + 1) * 512],
                                             start=first and part == 0, stop=last_tile and part == 1)
                    nc.tensor.matmul(misc[0:R, 0:P], gt[:, :], gn[:, :],
                                     start=first, stop=last_tile).then_inc(g_mm, 1)

                def one(s, b, p):
                    pe.wait_ge(g_blk, b + 1)
                    tile(s, b * NT, True, False)
                    with pe.Fori(1, NT - 1) as t:
                        tile(s, b * NT + t, False, False)
                    tile(s, b * NT + NT - 1, False, True)
                    pe_node(pe, b, p)
                    pe_out(pe, b, p)
                for s in range(0, NB - 1, SEG):
                    with pe.Fori(0, SEG // 2) as i:
                        one(s, s + 2 * i, 0)
                        one(s, s + 2 * i + 1, 1)
                one(NB - 1, NB - 1, 0)

        @block.vector
        def _(dve):
            steps = [0]

            def own(ins):
                ins.then_inc(vstep, 1)
                steps[0] += 1

            def settle():
                dve.wait_ge(vstep, steps[0])

            nc.vector.memset(xs[:, NB - 1, :], 0.0)
            nc.vector.memset(vv[:, 1, :], 1.0)
            for row, value in ((CH - 1, 0), (2 * CH - 1, N - 1), (3 * CH - 1, PADTYPE), (3 * CH, PADTYPE)):
                last = nc.vector.memset(meta_i[:, row, :], value)
            last.then_inc(xpad_set, 1)
            own(nc.vector.memset(nt_row[32:64, N:NB * P], PADTYPE))
            def chunk(c):
                dve.wait_ge(x_in[c], 32 if c == 4 else 16)
                for b in range(5 * c, 5 * c + 5):
                    own(nc.vector.bn_stats(stats[:, b, :], xs[:, b, :]))
                settle()
                for b in range(5 * c, 5 * c + 5):
                    own(nc.vector.bn_aggr(mv[:, b, :], stats[:, b, :]))

            def variance(part):
                settle()
                nc.vector.tensor_scalar(vv[:, 0, PARTS[part]], mv[:, PARTS[part], 1], 1e-5, None,
                                        ALU.add).then_inc(var_ready, 1)

            def inverse(part):
                bb = PARTS[part]
                var, r, t = (vv[:, k, bb] for k in range(3))
                dve.wait_ge(var_ready, part + 1)
                dve.wait_ge(std_ready, part + 1)
                own(nc.vector.reciprocal(r, t))
                settle()
                own(nc.vector.scalar_tensor_tensor(t, r, -0.5 * H_SCALE, r, ALU.mult, ALU.mult))
                settle()
                own(nc.vector.tensor_tensor(t, t, var, ALU.mult))
                settle()
                own(nc.vector.scalar_tensor_tensor(rstd[:, bb], t, 1.5 * H_SCALE, r, ALU.add, ALU.mult))
                settle()
                nc.vector.scalar_tensor_tensor(nmr[:, bb], mv[:, bb, 0], -1.0, rstd[:, bb],
                                               ALU.mult, ALU.mult).then_inc(rstd_ready, 1)

            def split(c):
                bb = slice(5 * c, 5 * c + 5)
                dve.wait_ge(relu_done, c + 1)
                if c < 2:
                    own(nc.vector.tensor_copy(hh[:, bb, 0:D], hf[:, bb, :]))
                    settle()
                else:
                    dve.wait_ge(hi_done, c - 1)
                nc.vector.tensor_tensor(hh[:, bb, D:2 * D], hf[:, bb, :], hh[:, bb, 0:D],
                                        ALU.subtract).then_inc(h_ready, 1)
            for c in range(3):
                chunk(c)
            variance(0)
            chunk(3)
            inverse(0)
            chunk(4)
            variance(1)
            dve.wait_ge(meta_in, 16 * 11)
            nc.vector.tensor_copy(meta_f[:, :, :], meta_i[:, :, :]).then_inc(meta_cast, 1)
            inverse(1)
            dve.wait_ge(rstd_ready, 2)
            for b in range(20, 25):
                own(nc.vector.tensor_scalar(hf[:, b, :], xs[:, b, :], mv[:, b, 0:1], rstd[:, b:b + 1],
                                            ALU.subtract, ALU.mult))
            settle()
            own(nc.vector.tensor_scalar(hh[:, 20:25, 0:D], hf[:, 20:25, :], 0.0, None, ALU.max))
            settle()
            nc.vector.scalar_tensor_tensor(hh[:, 20:25, D:2 * D], hf[:, 20:25, :], 0.0, hh[:, 20:25, 0:D],
                                           ALU.max, ALU.subtract).then_inc(h_ready, 1)
            for c in range(4):
                split(c)
            dve.wait_ge(dst_out, 1)
            dve.wait_ge(base_bc, 1)
            base_b = acc[3][:, 0:TC // 2]
            own(nc.vector.tensor_tensor(rel[:, :].rearrange("p (j a) -> p j a", a=2),
                                        dst_t[:, :].rearrange("p (j a) -> p j a", a=2),
                                        base_b[:, :].unsqueeze(2).to_broadcast([P, TC // 2, 2]), ALU.subtract))
            own(nc.vector.tensor_tensor(relq[:, :].rearrange("p (j a) -> p j a", a=4),
                                        dst_t[:, 0:4 * QUADS].rearrange("p (j a) -> p j a", a=4),
                                        base_b[:, 0:2 * QUADS:2].unsqueeze(2).to_broadcast([P, QUADS, 4]),
                                        ALU.subtract))
            V1 = 2 * PAIRS
            V2 = V1 + 4 * QUADS
            V3 = V2 + PAIRS
            V4 = V3 + QUADS - 2
            dve.wait_ge(consts, 6)
            own(nc.vector.tensor_tensor(viol[:, V2:V3], base_b[:, 0:PAIRS], pair16[:, :], ALU.subtract))
            own(nc.vector.tensor_copy(quad_f[:, :], base_b[:, 0:2 * QUADS:2]))
            settle()
            own(nc.vector.tensor_tensor(viol[:, V3:V4], quad_f[:, 2:QUADS], quad_f[:, 0:QUADS - 2],
                                        ALU.subtract))
            settle()

            def in_range(cols, values, low, high):
                own(nc.vector.tensor_scalar(viol[:, cols], values, -0.5 * (low + high), 2.0 / (high - low + 1),
                                            ALU.add, ALU.mult))
            in_range(slice(0, V1 // 2), rel[:, 0:V1:2], 0, W0 - 1)
            in_range(slice(V1 // 2, V1), rel[:, 1:V1:2], 0, W - 1)
            in_range(slice(V1, V2), relq[:, :], 0, WQ - 1)
            in_range(slice(V2, V3), viol[:, V2:V3], -16 * LATE, AHEAD)
            in_range(slice(V3, V4), viol[:, V3:V4], WQ, 2 * N)
            settle()
            own(nc.vector.tensor_reduce(nviol[:, 0:1], viol[:, 0:V4], AX.X, ALU.max, apply_absolute_value=True))
            settle()
            nc.vector.tensor_scalar(nviol[:, 1:2], nviol[:, 0:1], 1.0, None, ALU.is_gt).then_inc(viol_ready, 1)
            dve.wait_ge(viol_sum, 1)
            nc.vector.tensor_copy(flag[:, :], misc[0:1, 256:257]).then_inc(flag_ready, 1)
            own(nc.vector.tensor_copy(base_i[:, :], dst_t[0:1, 0:TC:2]))
            own(nc.vector.tensor_copy(quad_i[:, :], dst_t[0:1, 0:4 * QUADS:4]))
            settle()
            own(nc.vector.tensor_scalar(ring_i[:, :], base_i[:, :], RING - 1, None, ALU.bitwise_and))
            dve.wait_ge(et_out, 3)
            own(nc.vector.scalar_tensor_tensor(seg[:, 0:TC:2], et_t[:, 0:TC:2], float(W0), rel[:, 0:TC:2],
                                               ALU.mult, ALU.add))
            settle()
            nc.vector.scalar_tensor_tensor(seg[:, 1:TC:2], et_t[:, 1:TC:2], float(W), rel[:, 1:TC:2],
                                           ALU.mult, ALU.add).then_inc(seg_ready, 1)
            own(nc.vector.tensor_tensor(wmask[:, :, :], nt_t[:, :].unsqueeze(2).to_broadcast([P, NB, K]),
                                        iota_w[:, 0:K].unsqueeze(1).to_broadcast([P, NB, K]), ALU.is_equal))
            dve.wait_ge(ntrow_in, 16)
            dve.wait_ge(zeroed_s, 2)
            own(nc.vector.tensor_scalar(bsel[32:32 + K, :], nt_row[32:32 + K, :], kcol[32:32 + K, :], None,
                                        ALU.is_equal))
            settle()
            dve.sem_inc(mask_ready, 1)
            for s in (scaled, fin, os_free, row_used):
                dve.sem_inc(s, 2)
            for s in (c_out, c_out_v, g_blk):
                dve.sem_inc(s, 1)
            dve.wait_ge(flag_ready, 1)
            bad = dve.value_load(flag[0:1, 0:1], min_val=0, max_val=FLAG_MAX)

            def rc_of(rc, ind, count, steps_before, done):
                nc.vector.tensor_scalar(ind, count, 1.0, None, ALU.min).then_inc(cvec, 1)
                nc.vector.tensor_scalar(rc, count, 1.0, H_SCALE, ALU.max, ALU.mult).then_inc(cvec, 1)
                dve.wait_ge(cvec, steps_before + 2)
                nc.vector.reciprocal(rc, rc).then_inc(done, 1)

            with dve.If(bad < 1):
                DVE = mybir.EngineType.DVE
                def count_oh(batch, q):
                    c0 = batch * 4 * CB
                    for one_hots, column, n in ((tcnt, et16, R), (ncnt, relq, WQ)):
                        last = nc.vector.tensor_tensor(
                            one_hots[:, q, :, :],
                            column[:, bass.ds(c0, 4 * CB)].unsqueeze(1).to_broadcast([P, n, 4 * CB]),
                            count_of[:, 0:n, :], ALU.is_equal)
                    last.then_inc(c_oh, 1)

                def count_out(q, at):
                    for v in range(CA, CB):
                        last = nc.vector.tensor_copy(cnt_q[(q + v) % 2][:, bass.ds(at[v - CA], WQ)],
                                                     acc[q][0:R, v * WQ:(v + 1) * WQ])
                    last.then_inc(c_out_v, 1)

                dve.wait_ge(count_set, 1)
                dve.wait_ge(cnt_zeroed, 2)
                count_oh(0, 0)
                count_oh(1, 1)
                with dve.Fori(1, CITERS) as i:
                    for q in range(2):
                        at = windows(quad_i, (2 * i + q - 2) * CB + CA, CB - CA, DVE)
                        dve.wait_ge(c_mm, 2 * i + q)
                        count_oh(2 * i + q, q)
                        count_out(q, at)
                for q in range(2):
                    batch = 2 * CITERS - 2 + q
                    at = windows(quad_i, batch * CB + CA, CB - CA, DVE)
                    dve.wait_ge(c_mm, batch + 2)
                    count_out(q, at)

                def onehot(o, cols):
                    for a, width in ((0, R * W0), (1, R * W)):
                        last = nc.vector.tensor_scalar(oh[:, o, a, 0:width], iota_w[:, 0:width], cols[:, a:a + 1],
                                                       None, ALU.is_equal)
                    last.then_inc(oh_ready, 1)

                def add(pair, bank, at, adds):
                    dve.wait_ge(pair_mm, BODY + pair + 1)
                    dve.wait_ge(s_add, adds)
                    span = S[:, :, bass.ds(at, W)]
                    nc.vector.tensor_tensor(span, span,
                                            acc[bank][:, 0:R * W].rearrange("p (t n) -> p t n", n=W),
                                            ALU.add).then_inc(s_add, 1)
                dve.wait_ge(seg_ready, 1)
                dve.wait_ge(c_mm, 2 * CITERS + 1)
                onehot(1, seg[:, 0:2])
                onehot(2, seg[:, 2:4])
                onehot(3, seg[:, 4:6])
                at = windows(ring_i, 0, LATE, DVE)
                dve.wait_ge(staged, 1)
                for j in range(LATE):
                    onehot(j, seg_s[:, 2 * j:2 * j + 2])
                    add(j, j, at[j], j)
                dve.wait_ge(c_out, 2 * CITERS + 1)
                dve.wait_ge(c_out_v, 2 * CITERS + 1)
                dve.wait_ge(cnt_zeroed, 2)
                nc.vector.tensor_tensor(cnt[:, 0:NB * P], cnt[:, 0:NB * P], cnt_q[1][:, 0:NB * P],
                                        ALU.add).then_inc(cnt_ready, 1)
                dve.wait_ge(cnt_ready, 1)
                nc.vector.tensor_scalar(bsel[0:R, :], cnt[:, 0:NB * P], 1.0, None, ALU.min).then_inc(ind_ready, 1)
                dve.wait_ge(count_set, 2)
                dve.wait_ge(cnt_moved, 32)
                nc.vector.tensor_scalar(rc_w, rc_w, 1.0, H_SCALE, ALU.max, ALU.mult).then_inc(cvec, 1)
                dve.wait_ge(cvec, 1)
                nc.vector.reciprocal(rc_w, rc_w).then_inc(rc_ready, 1)

                def body(i, first):
                    n0 = LATE + i * PER
                    done = 0
                    for u in range(BODY):
                        pair = LATE + i * BODY + u
                        g, v = u // PPB, u % PPB
                        if u % 4 == 0:
                            at = windows(ring_i, LATE + i * BODY + u, 4, DVE)
                        if u == BODY // 2 - 3:
                            dve.wait_ge(staged, 2 * i + 2)
                        if u == BODY - 3:
                            dve.wait_ge(staged, 2 * i + 3)
                        w = (u + 3) % BODY
                        onehot(w % 4, seg_s[:, 2 * w:2 * w + 2])
                        if v in (1, 2, 3):
                            dve_fetch(dve, 4 * i + g, g % 2, 2 * i + g // 2, v - 1)
                        add(pair, (u + LATE) % 4, at[u % 4], n0 + done)
                        done += 1
                        if u == BODY - 1:
                            dve.wait_ge(zeroed, 4 * i + g + 1)
                            dve.wait_ge(s_add, n0 + done)
                            nc.vector.tensor_tensor(S[:, :, 0:W], S[:, :, 0:W], S[:, :, RING:RING + W],
                                                    ALU.add).then_inc(s_add, 1)
                            done += 1
                            dve.wait_ge(s_add, n0 + done)
                            nc.vector.memset(S[:, :, RING:RING + W], 0.0).then_inc(s_add, 1)
                            done += 1
                        if v == PPB - 1:
                            dve.wait_ge(s_add, n0 + done)
                            dve_scale(dve, 4 * i + g, g % 2, g, 2 * i + g // 2)
                        if v == 5 and not (first and g == 0):
                            dve_finish(dve, 4 * i + g - 1, (g - 1) % 2)
                    assert done == PER
                body(0, True)
                with dve.Fori(1, ITERS) as i:
                    body(i, False)
                at = windows(ring_i, PAIRS - 1, 1, DVE)
                add(PAIRS - 1, (PAIRS - 1) % 4, at[0], LATE + ITERS * PER)
                dve.wait_ge(s_add, LATE + ITERS * PER + 1)
                dve_scale(dve, NB - 1, 0, 0, (NB - 1) // 2, NLAST)
                dve_finish(dve, NB - 2, 1)
                dve_finish(dve, NB - 1, 0, misc, NLAST)
            with dve.Else():
                nc.vector.memset(bbase[:, 0:1], 0.0).then_inc(g_vec, 1)
                GV = 6

                def tile(b, t):
                    n = b * NT + t
                    v0 = 1 + b + n * GV

                    def done(k):
                        dve.wait_ge(g_vec, v0 + k)
                    dve.wait_ge(g_mm, n + 1)
                    done(0)
                    d, v, lo, hi, col = (gcol[:, k:k + 1] for k in range(5))
                    nc.vector.tensor_tensor(v, dst_t[:, bass.ds(t, 1)], bbase[:, 0:1],
                                            ALU.subtract).then_inc(g_vec, 1)
                    done(1)
                    nc.vector.tensor_scalar(lo, v, 0.0, None, ALU.is_ge).then_inc(g_vec, 1)
                    nc.vector.tensor_scalar(hi, v, float(P), None, ALU.is_lt).then_inc(g_vec, 1)
                    nc.vector.scalar_tensor_tensor(col, et_t[:, bass.ds(t, 1)], float(P), v,
                                                   ALU.mult, ALU.add).then_inc(g_vec, 1)
                    done(4)
                    nc.vector.scalar_tensor_tensor(d, col, 1.0, lo, ALU.add, ALU.mult).then_inc(g_vec, 1)
                    done(5)
                    nc.vector.tensor_tensor(d, d, hi, ALU.mult).then_inc(g_vec, 1)
                    done(6)
                    nc.vector.tensor_scalar(goh[:, :], iota1[:, :], d, None, ALU.is_equal)
                    nc.vector.tensor_scalar(gn[:, :], iota_w[:, 0:P], v, None, ALU.is_equal)
                    nc.vector.tensor_scalar(gt[:, :], iota_w[:, 0:R], et_t[:, bass.ds(t, 1)], None,
                                            ALU.is_equal).then_inc(g_oh, 1)

                def one(b, p, use):
                    with dve.Fori(0, NT) as t:
                        tile(b, t)
                    dve.wait_ge(g_mm, (b + 1) * NT + 1)
                    dve.wait_ge(zeroed, b + 1)
                    for q in range(4):
                        nc.vector.tensor_copy(S[:, 4 * q:4 * q + 4, p * P:(p + 1) * P],
                                              acc[q][:, :].rearrange("p (t n) -> p t n", n=P)
                                              ).then_inc(s_add, 1)
                    rc_of(grc[:, :], bsel[0:R, bass.ds(b * P, P)], misc[0:R, 0:P], 2 * b, g_rc)
                    dve.wait_ge(s_add, 4 * b + 4)
                    nc.vector.tensor_scalar(bbase[:, 0:1], bbase[:, 0:1], float(P), None,
                                            ALU.add).then_inc(g_vec, 1)
                    dve.sem_inc(g_blk, 1)
                    dve_scale(dve, b, p, p, use)
                    dve_finish(dve, b, p)
                with dve.Fori(0, (NB - 1) // 2) as i:
                    one(2 * i, 0, i)
                    one(2 * i + 1, 1, i)
                one(NB - 1, 0, (NB - 1) // 2)


_INS = ['x', 'src', 'dst', 'edge_type_16', 'node_type_8', 'L0_gnn_W_edge', 'L0_gnn_b_edge', 'L0_gnn_W_node',
        'L0_gnn_b_node']


def kernel(**inputs):
    import numpy as _np
    import concourse.bacc as _bacc
    from concourse import mybir as _mybir
    from concourse.bass_utils import run_bass_kernel_spmd as _run

    nc = _bacc.Bacc("TRN2", target_bir_lowering=False, num_devices=1)
    arrays, args = {}, []
    for name in _INS:
        a = _np.ascontiguousarray(inputs[name])
        arrays[f"in_{name}_dram"] = a
        args.append(nc.dram_tensor(f"in_{name}_dram", a.shape, _mybir.dt.from_np(a.dtype), kind="ExternalInput").ap())
    n, d = inputs['x'].shape
    args.append(nc.dram_tensor("out_0_dram", (n, d), _mybir.dt.float32, kind="ExternalOutput").ap())
    gnn_layer(nc, *args)
    r = _run(nc, [arrays], core_ids=[0])
    return r.results[0]["out_0_dram"]
```
